# Optimizing a Trainium2 kernel written in Bass

```python
import numpy as np
import jax
import jax.numpy as jnp

def _softmax(x, axis=-1):
    return jax.nn.softmax(x, axis=axis)

def _gelu(x):
    return jax.nn.gelu(x, approximate=True)

def _silu(x):
    return jax.nn.silu(x)

def _sigmoid(x):
    return jax.nn.sigmoid(x)

def _layernorm(x, axis=-1, eps=1e-05):
    m = jnp.mean(x, axis=axis, keepdims=True)
    v = jnp.var(x, axis=axis, keepdims=True)
    return (x - m) / jnp.sqrt(v + eps)

def _scatter_add(tgt, idx, src, axis=0):
    return tgt.at[idx].add(src)

def _segment_sum(src, seg, n):
    return jax.ops.segment_sum(src, seg, n)
kernel_name = 'mk_decoder_preln_d1_seqx_r8_5bb291'

def setup_inputs(seed: int=0):
    np.random.seed(seed)
    _w = jnp.asarray

    def _rec_inputs():
        import jax
        import jax.numpy as jnp
        _rk = jax.random.key(seed)
        x = -0.0002928 + 1 * jax.random.normal(jax.random.fold_in(_rk, 1), (8, 256, 128), jnp.float32)
        _lenS = 256 - jax.random.randint(jax.random.fold_in(_rk, 7), (8,), 0, max(1, 256 // 4) + 1, jnp.int32)
        _lenS2 = 256 - jax.random.randint(jax.random.fold_in(_rk, 8), (8,), 0, max(1, 256 // 4) + 1, jnp.int32)
        _ctx_1024P = jax.random.normal(jax.random.fold_in(_rk, 11), (8, 16, 128), jnp.float32)
        _ctx_1024c = jax.random.dirichlet(jax.random.fold_in(_rk, 511), 0.3 * jnp.ones((16,), jnp.float32), (8, 256))
        _ctx_1024t = jnp.einsum('bsk,bkd->bsd', _ctx_1024c, _ctx_1024P)
        _ctx_1024t = _ctx_1024t * jax.lax.rsqrt(jnp.mean(jnp.square(_ctx_1024t)) + 1e-12) * 0.953939
        ctx_1024 = -1.39393e-06 + 0.999914 * (_ctx_1024t + 0.3 * jax.random.normal(jax.random.fold_in(_rk, 611), (8, 256, 128), jnp.float32))
        return (x, ctx_1024)
    x, ctx_1024 = _rec_inputs()

    def _L0_attn_setup():
        import jax, jax.numpy as jnp
        import numpy as np
        DIM = 128
        HEADS = 16
        DIM_HEAD = 64
        DIM_INNER = HEADS * DIM_HEAD
        SCALE = DIM_HEAD ** (-0.5)

        def rmsnorm(x, w):
            eps = jnp.asarray(jnp.finfo(x.dtype).eps, x.dtype)
            var = jnp.mean(jnp.square(x), axis=-1, keepdims=True)
            return x * jax.lax.rsqrt(var + eps) * w
        key = jax.random.key(seed)
        ks = jax.random.split(key, 6)
        tokens = jax.random.normal(ks[0], (2, 256, DIM), dtype=jnp.float32)
        norm_w = jnp.ones((DIM,), dtype=jnp.float32)
        Wq = jax.random.normal(ks[1], (DIM, DIM_INNER), dtype=jnp.float32) * 0.02
        Wkv = jax.random.normal(ks[2], (DIM, 2 * DIM_INNER), dtype=jnp.float32) * 0.02
        Wout = jax.random.normal(ks[3], (DIM_INNER, DIM), dtype=jnp.float32) * 0.02
        Wg = jax.random.normal(ks[4], (DIM, HEADS), dtype=jnp.float32) * 0.02
        return {'tokens': tokens, 'norm_w': norm_w, 'Wq': Wq, 'Wkv': Wkv, 'Wout': Wout, 'Wg': Wg}
    _L0_attn_all = _L0_attn_setup()
    _L0_attn_in = {k: v for k, v in _L0_attn_all.items() if k in ('norm_w', 'Wq', 'Wkv', 'Wout', 'Wg')}
    del _L0_attn_all

    def _L0_xattn_setup():
        import jax, jax.numpy as jnp
        import numpy as np
        import math
        HIDDEN = 128
        HEADS = 16
        HEAD = HIDDEN // HEADS
        SCALE_BASE = 512.0

        def _gammas(heads):
            return 1.0 - jnp.exp(jnp.linspace(math.log(1.0 / 32.0), math.log(1.0 / 512.0), heads))

        def _xpos(x, downscale):
            S, d = (x.shape[2], x.shape[3])
            half = d // 2
            base_scale = (jnp.arange(0, d, 2, dtype=jnp.float32) + 0.4 * d) / (1.4 * d)
            pos = jnp.arange(S, dtype=jnp.float32)
            scale = base_scale[None, :] ** (pos / SCALE_BASE)[:, None]
            if downscale:
                scale = 1.0 / scale
            inv_freq = 1.0 / 10000.0 ** (jnp.arange(half, dtype=jnp.float32) / half)
            sinusoid = pos[:, None] * inv_freq[None, :]
            sin = jnp.repeat(jnp.sin(sinusoid) * scale, 2, axis=-1)
            cos = jnp.repeat(jnp.cos(sinusoid) * scale, 2, axis=-1)
            x1 = x[..., ::2]
            x2 = x[..., 1::2]
            rot = jnp.stack([-x2, x1], axis=-1).reshape(x.shape)
            return x * cos + rot * sin

        def _decay_mask(S, gammas):
            n = jnp.arange(S)[:, None]
            m = jnp.arange(S)[None, :]
            diff = (n - m).astype(jnp.float32)
            mask = n >= m
            pw = jnp.maximum(diff, 0.0)[None, :, :]
            return jnp.where(mask[None, :, :], gammas[:, None, None] ** pw, 0.0)

        def retention_forward(Q, K, V):
            B, S, _ = Q.shape

            def split(x, hd):
                return x.reshape(B, S, HEADS, hd).transpose(0, 2, 1, 3)
            q = _xpos(split(Q, HEAD), downscale=False)
            k = _xpos(split(K, HEAD), downscale=True)
            v = split(V, HEAD)
            D = _decay_mask(S, _gammas(HEADS).astype(Q.dtype))
            scores = jnp.einsum('bhsd,bhtd->bhst', q, k) * D[None]
            out = jnp.einsum('bhst,bhtd->bhsd', scores, v)
            return out.transpose(0, 2, 1, 3).reshape(B, S, HEADS * HEAD)
        key = jax.random.key(seed)
        kq, kk, kv = jax.random.split(key, 3)
        B, S = (2, 256)
        return {'Q': jax.random.normal(kq, (B, S, HIDDEN), dtype=jnp.float32), 'K': jax.random.normal(kk, (B, S, HIDDEN), dtype=jnp.float32), 'V': jax.random.normal(kv, (B, S, HIDDEN), dtype=jnp.float32)}
    _L0_xattn_all = _L0_xattn_setup()
    _L0_xattn_in = {k: v for k, v in _L0_xattn_all.items() if k in ()}
    del _L0_xattn_all

    def _L0_ffn_setup():
        import jax, jax.numpy as jnp
        import numpy as np
        D = 128
        H = 512
        E = 12
        K = 3
        B, S = (1, 256)
        key = jax.random.key(seed)
        ks = jax.random.split(key, 6)
        scale = 0.02
        x = jax.random.normal(ks[0], (B, S, D), dtype=jnp.float32)
        Wg = jax.random.normal(ks[1], (D, E), dtype=jnp.float32) * scale
        Wup = jax.random.normal(ks[2], (E, D, H), dtype=jnp.float32) * scale
        bup = jax.random.normal(ks[3], (E, H), dtype=jnp.float32) * scale
        Wdown = jax.random.normal(ks[4], (E, H, D), dtype=jnp.float32) * scale
        bdown = jax.random.normal(ks[5], (E, D), dtype=jnp.float32) * scale
        return {'x': x, 'Wg': Wg, 'Wup': Wup, 'bup': bup, 'Wdown': Wdown, 'bdown': bdown}
    _L0_ffn_all = _L0_ffn_setup()
    _L0_ffn_in = {k: v for k, v in _L0_ffn_all.items() if k in ('Wg', 'Wup', 'bup', 'Wdown', 'bdown')}
    del _L0_ffn_all
    return {'x': x, 'ctx_1024': ctx_1024, 'L0_attn_norm_w': _L0_attn_in['norm_w'], 'L0_attn_Wq': _L0_attn_in['Wq'], 'L0_attn_Wkv': _L0_attn_in['Wkv'], 'L0_attn_Wout': _L0_attn_in['Wout'], 'L0_attn_Wg': _L0_attn_in['Wg'], 'L0_ffn_Wg': _L0_ffn_in['Wg'], 'L0_ffn_Wup': _L0_ffn_in['Wup'], 'L0_ffn_bup': _L0_ffn_in['bup'], 'L0_ffn_Wdown': _L0_ffn_in['Wdown'], 'L0_ffn_bdown': _L0_ffn_in['bdown']}

def reference(x, ctx_1024, L0_attn_norm_w, L0_attn_Wq, L0_attn_Wkv, L0_attn_Wout, L0_attn_Wg, L0_ffn_Wg, L0_ffn_Wup, L0_ffn_bup, L0_ffn_Wdown, L0_ffn_bdown):
    import jax
    import jax.numpy as jnp

    def _L0_attn_ref(tokens, norm_w, Wq, Wkv, Wout, Wg):
        import jax, jax.numpy as jnp
        import numpy as np
        DIM = 128
        HEADS = 16
        DIM_HEAD = 64
        DIM_INNER = HEADS * DIM_HEAD
        SCALE = DIM_HEAD ** (-0.5)

        def rmsnorm(x, w):
            eps = jnp.asarray(jnp.finfo(x.dtype).eps, x.dtype)
            var = jnp.mean(jnp.square(x), axis=-1, keepdims=True)
            return x * jax.lax.rsqrt(var + eps) * w
        b, n, _ = tokens.shape
        x = rmsnorm(tokens, norm_w)
        q = x @ Wq
        kv = x @ Wkv
        k, v = jnp.split(kv, 2, axis=-1)

        def split_heads(t):
            return t.reshape(b, n, HEADS, DIM_HEAD).transpose(0, 2, 1, 3)
        q, k, v = map(split_heads, (q, k, v))
        sim = jnp.einsum('bhid,bhjd->bhij', q, k) * SCALE
        causal_mask = jnp.triu(jnp.ones((n, n), dtype=bool), k=1)
        sim = jnp.where(causal_mask, jnp.asarray(-jnp.finfo(sim.dtype).max, sim.dtype), sim)
        attn = jax.nn.softmax(sim, axis=-1)
        out = jnp.einsum('bhij,bhjd->bhid', attn, v)
        gates = jax.nn.sigmoid(x @ Wg)
        gates = gates.transpose(0, 2, 1)[..., None]
        out = gates * out
        out = out.transpose(0, 2, 1, 3).reshape(b, n, DIM_INNER)
        return out @ Wout

    def _L0_xattn_ref(Q, K, V):
        import jax, jax.numpy as jnp
        import numpy as np
        import math
        HIDDEN = 128
        HEADS = 16
        HEAD = HIDDEN // HEADS
        SCALE_BASE = 512.0

        def _gammas(heads):
            return 1.0 - jnp.exp(jnp.linspace(math.log(1.0 / 32.0), math.log(1.0 / 512.0), heads))

        def _xpos(x, downscale):
            S, d = (x.shape[2], x.shape[3])
            half = d // 2
            base_scale = (jnp.arange(0, d, 2, dtype=jnp.float32) + 0.4 * d) / (1.4 * d)
            pos = jnp.arange(S, dtype=jnp.float32)
            scale = base_scale[None, :] ** (pos / SCALE_BASE)[:, None]
            if downscale:
                scale = 1.0 / scale
            inv_freq = 1.0 / 10000.0 ** (jnp.arange(half, dtype=jnp.float32) / half)
            sinusoid = pos[:, None] * inv_freq[None, :]
            sin = jnp.repeat(jnp.sin(sinusoid) * scale, 2, axis=-1)
            cos = jnp.repeat(jnp.cos(sinusoid) * scale, 2, axis=-1)
            x1 = x[..., ::2]
            x2 = x[..., 1::2]
            rot = jnp.stack([-x2, x1], axis=-1).reshape(x.shape)
            return x * cos + rot * sin

        def _decay_mask(S, gammas):
            n = jnp.arange(S)[:, None]
            m = jnp.arange(S)[None, :]
            diff = (n - m).astype(jnp.float32)
            mask = n >= m
            pw = jnp.maximum(diff, 0.0)[None, :, :]
            return jnp.where(mask[None, :, :], gammas[:, None, None] ** pw, 0.0)

        def retention_forward(Q, K, V):
            B, S, _ = Q.shape

            def split(x, hd):
                return x.reshape(B, S, HEADS, hd).transpose(0, 2, 1, 3)
            q = _xpos(split(Q, HEAD), downscale=False)
            k = _xpos(split(K, HEAD), downscale=True)
            v = split(V, HEAD)
            D = _decay_mask(S, _gammas(HEADS).astype(Q.dtype))
            scores = jnp.einsum('bhsd,bhtd->bhst', q, k) * D[None]
            out = jnp.einsum('bhst,bhtd->bhsd', scores, v)
            return out.transpose(0, 2, 1, 3).reshape(B, S, HEADS * HEAD)
        return retention_forward(Q, K, V)

    def _L0_ffn_ref(x, Wg, Wup, bup, Wdown, bdown):
        import jax, jax.numpy as jnp
        import numpy as np
        D = 128
        H = 512
        E = 12
        K = 3
        B, S = (1, 256)
        gate_logits = jnp.einsum('bsd,de->bse', x, Wg)
        topw, sel = jax.lax.top_k(gate_logits, K)
        topw = jax.nn.softmax(topw.astype(jnp.float32), axis=-1).astype(x.dtype)
        cw = jnp.einsum('bsk,bske->bse', topw, jax.nn.one_hot(sel, E, dtype=x.dtype))
        h = jax.nn.gelu(jnp.einsum('bsd,edh->ebsh', x, Wup) + bup[:, None, None, :], approximate=False)
        y = jnp.einsum('ebsh,ehd->ebsd', h, Wdown) + bdown[:, None, None, :]
        return jnp.einsum('bse,ebsd->bsd', cw, y)
    x = x + _L0_attn_ref(_layernorm(x, axis=-1), L0_attn_norm_w, L0_attn_Wq, L0_attn_Wkv, L0_attn_Wout, L0_attn_Wg)
    x = x + _L0_xattn_ref(_layernorm(x, axis=-1), ctx_1024, ctx_1024)
    x = x + _L0_ffn_ref(_layernorm(x, axis=-1), L0_ffn_Wg, L0_ffn_Wup, L0_ffn_bup, L0_ffn_Wdown, L0_ffn_bdown)
    return x

_drawn_inputs = setup_inputs


def setup_inputs(seed=0):
    import zlib

    import numpy as np

    out = dict(_drawn_inputs(seed))
    spreads = {'L0_attn_norm_w': (1.0, 0.6)}
    factors = {'L0_attn_Wq': 8.0,
     'L0_attn_Wkv': 8.0,
     'L0_attn_Wout': 8.0,
     'L0_attn_Wg': 8.0,
     'L0_ffn_Wg': 8.0,
     'L0_ffn_Wup': 8.0,
     'L0_ffn_bup': 64.0,
     'L0_ffn_Wdown': 8.0,
     'L0_ffn_bdown': 200.0}
    for name, (base, spread) in spreads.items():
        noise = np.random.default_rng([zlib.crc32(name.encode()), seed]).standard_normal(out[name].shape)
        drawn = base * np.exp(spread * noise) if base else spread * noise
        out[name] = jnp.asarray(drawn.astype(out[name].dtype))
    for name, factor in factors.items():
        out[name] = (out[name] * factor).astype(out[name].dtype)
    return out
```

```python
from contextlib import ExitStack

import numpy as np

import concourse.bass as bass
from concourse import mybir

F32 = mybir.dt.float32
BF16 = mybir.dt.bfloat16
I32 = mybir.dt.int32
ALU = mybir.AluOpType
ACT = mybir.ActivationFunctionType
AX = mybir.AxisListType

P = 128
B, S, D = 8, 256, 128
T = S // P
NT = B * T
H, DH = 16, 64
PAIRS = H // 2
VW = DH + 1
BLOCKS = 3
RH, RD = 16, 8
HALF = RH * RD * RD // 2
E, HID, TOPK = 12, 512, 3
HC = HID // P
CHUNK = 512
SCALE = DH ** -0.5
NEG = -3.0e38
FOUND = 3.0e38
LN_EPS = 1e-5
RMS_EPS = float(np.finfo(np.float32).eps)
MAGIC = float(0x5F3759DF)
MAX8 = 8
LGW = E + MAX8


def retention_tables():
    half = RD // 2
    base = (np.arange(0, RD, 2, dtype=np.float32) + np.float32(0.4 * RD)) / np.float32(1.4 * RD)
    pos = np.arange(S, dtype=np.float32)
    scale = base[None, :] ** (pos / np.float32(512.0))[:, None]
    inv = np.float32(1.0) / np.float32(10000.0) ** (np.arange(half, dtype=np.float32) / np.float32(half))
    angle = pos[:, None] * inv[None, :]
    gamma = np.float32(1.0) - np.exp(np.linspace(np.log(1 / 32), np.log(1 / 512), RH)).astype(np.float32)
    decay = gamma.astype(np.float64)[None, :] ** np.arange(S)[:, None]
    sign = np.tile([-1.0, 1.0], half)
    out = []
    for s, g in ((scale, decay), (1.0 / scale, 1.0 / decay)):
        for f, w in ((np.cos(angle), np.ones(RD)), (np.sin(angle), sign)):
            t = np.repeat(f.astype(np.float64) * s, 2, axis=1) * w
            out.append((g[:, :, None] * t[:, None, :]).reshape(S, RH * RD))
    return np.stack(out).reshape(4, T, P, D).transpose(2, 0, 1, 3).astype(np.float32).copy()


def bc(ap, dim, n):
    shape = list(ap.shape)
    return ap.unsqueeze(dim).broadcast_to(shape[:dim] + [n] + shape[dim:])


def decoder(nc, x, ctx, norm_w, wq, wkv, wout, wg, f_wg, f_wup, f_bup, f_wdown, f_bdown, tables, out):
    with ExitStack() as stack:
        def sb(name, shape, dt=F32):
            return stack.enter_context(nc.sbuf_tensor(name, shape, dt))

        def bank(name):
            return stack.enter_context(nc.psum_tensor(name, [P, 512], F32))

        def sem(name):
            return stack.enter_context(nc.semaphore(name))

        x_all = sb("x_all", [P, NT, D])
        xn3T_all = sb("xn3T_all", [P, NT * P])
        cw_all = sb("cw_all", [P, NT, E])
        wq_sb = sb("wq_sb", [P, H * DH])
        wkv_sb = sb("wkv_sb", [P, 2 * H * DH])
        wout_sb = sb("wout_sb", [P, PAIRS, D])
        wg_sb = sb("wg_sb", [P, H])
        fwg_sb = sb("fwg_sb", [P, E])
        normw_sb = sb("normw_sb", [P, 1])
        tab = sb("tab", [P, 4, T, D])
        bup_sb = sb("bup_sb", [P, E, HC])
        bup_rows = sb("bup_rows", [E * HC, P])
        bdown_sb = sb("bdown_sb", [E, D])
        wT = sb("wT", [P, 2, 2, P])
        a_sb = sb("a_sb", [P, H, P])
        ident = sb("ident", [P, P])
        ident16 = sb("ident16", [P, P], BF16)
        mask16 = sb("mask16", [P, 2, P], BF16)
        tri = sb("tri", [P, P])
        ones = sb("ones", [P, P])
        st6 = sb("st6", [P, NT, 6])
        mv = sb("mv", [P, NT, 2])
        rs1 = sb("rs1", [P, NT])
        r_ln = sb("r_ln", [P, NT])
        ms = sb("ms", [P, NT])
        nwt = sb("nwt", [P, NT])
        nwa = sb("nwa", [P, NT])
        nwy = sb("nwy", [P, NT])
        xrn = sb("xrn", [P, T, D])
        xT = sb("xT", [P, S])
        gexp = sb("gexp", [P, T, H])
        gate1 = sb("gate1", [P, T, H])
        gate = sb("gate", [P, T, H])
        v_sb = sb("v_sb", [P, T, H, VW])
        z_sb = sb("z_sb", [P, 2, S])
        mx = sb("mx", [P, 2, 2, 2])
        nmx = sb("nmx", [P, 2, 2, 2])
        p_sb = sb("p_sb", [P, 2, 2, BLOCKS * P])
        pT = sb("pT", [P, 2, 2, BLOCKS * P])
        rr = sb("rr", [P, T, 2])
        rg = sb("rg", [P, T, 2])
        o_sb = sb("o_sb", [P, 2, T, P])
        oT = sb("oT", [P, PAIRS, T, P])
        x1b = sb("x1b", [P, T, D])
        x2b = sb("x2b", [P, T, D])
        bst = sb("bst", [P, T, 6])
        bmv = sb("bmv", [P, T, 2])
        brs = sb("brs", [P, T])
        xn2 = sb("xn2", [P, T, D])
        xn3 = sb("xn3", [P, T, D])
        xn3T = sb("xn3T", [P, S])
        ctx_b = sb("ctx_b", [P, T, D])
        kq1 = sb("kq1", [P, T, D])
        kq2 = sb("kq2", [P, T, D])
        kt = sb("kt", [P, T, D])
        qt = sb("qt", [P, T, D])
        kv = sb("kv", [P, T, 2, HALF])
        prod = sb("prod", [P, HALF])
        ret = sb("ret", [P, T, D])
        lg = sb("lg", [P, T, LGW])
        top = sb("top", [P, T, MAX8])
        pick = sb("pick", [P, T, MAX8])
        rep = sb("rep", [P, T, LGW])
        hit = sb("hit", [P, T, E])
        dl = sb("dl", [P, T, E])
        el = sb("el", [P, T, E])
        es = sb("es", [P, T])
        er = sb("er", [P, T])
        cwb = sb("cwb", [P, T, E])
        wup_sb = sb("wup_sb", [P, 2, HID])
        wdn_sb = sb("wdn_sb", [P, 2, HC, D])
        hT = sb("hT", [P, 2, HC, CHUNK])
        spare = sb("spare", [P, 1])
        bup_now = sb("bup_now", [P, 2, HC])
        cwT = sb("cwT", [E, 2, P])

        s1 = [bank("s1_even"), bank("s1_odd")]
        s0 = bank("s0")
        zb = bank("zb")
        tb = [bank("tb_a"), bank("tb_b")]
        ob = bank("ob")
        xb = bank("xb")

        pair_bank = [s1, [zb, ob]]

        ld_x, ld_w, ld_wo, ld_c, ld_ctx, stored = (
            sem(n) for n in ("ld_x", "ld_w", "ld_wo", "ld_c", "ld_ctx", "stored"))
        ld_e = [sem("ld_e_even"), sem("ld_e_odd")]
        consts = sem("consts")
        consts_v = sem("consts_v")
        pw_T, pw_A, aw_T, aw_A = sem("pw_T"), sem("pw_A"), sem("aw_T"), sem("aw_A")
        stat1 = sem("stat1")
        pe_S, pe_T, pe_PV, pe_OT, pe_Z, pe_XT, pe_G, pe_V, pe_OUT, pe_RET, pe_XN, pe_LG = (
            sem(n) for n in ("pe_S", "pe_T", "pe_PV", "pe_OT", "pe_Z", "pe_XT", "pe_G", "pe_V", "pe_OUT",
                             "pe_RET", "pe_XN", "pe_LG"))
        v_nm, v_PT, v_norm, v_oT, v_V, v_x1, v_xn2, v_ret, v_x2, v_xn3, v_lg, v_dl, v_cw, v_xrn, v_chain = (
            sem(n) for n in ("v_nm", "v_PT", "v_norm", "v_oT", "v_V", "v_x1", "v_xn2", "v_ret", "v_x2", "v_xn3",
                             "v_lg", "v_dl", "v_cw", "v_xrn", "v_chain"))
        a_P, a_z, a_PT, a_V, a_xT, a_ge, a_xn3T, a_el = (
            sem(n) for n in ("a_P", "a_z", "a_PT", "a_V", "a_xT", "a_ge", "a_xn3T", "a_el"))
        p_kv, p_q, p_keep, p_chain = (sem(n) for n in ("p_kv", "p_q", "p_keep", "p_chain"))
        f_bias, f_cT, f_cs, f_b, f_acc, f_up, f_gelu, f_dn, f_sum = (
            sem(n) for n in ("f_bias", "f_cT", "f_cs", "f_b", "f_acc", "f_up", "f_gelu", "f_dn", "f_sum"))

        def at(b, per, k):
            if isinstance(b, tuple):
                return b[0] * per + (b[1] * per + k)
            return b * per + k

        def wait(eng, s, value):
            if not isinstance(value, int) or value > 0:
                eng.wait_ge(s, value)

        def back(b):
            return (b[0], b[1] - 1) if isinstance(b, tuple) else b - 1

        def tile_of(b, t):
            return (b[0] * T + (b[1] * T + t)) if isinstance(b, tuple) else b * T + t

        def batches(eng, head, body, tail):
            head(0)
            with eng.Fori(0, B - 1) as i:
                body((i, 1))
            tail(B - 1)

        def run(eng, step, prelude=None):
            def steps(b, first):
                for s in range(PAIRS):
                    step(b, None if first else back(b), s)

            def drain(b):
                for s in range(PAIRS):
                    step(None, b, s)
            if prelude:
                prelude()
            batches(eng, lambda b: steps(b, True), lambda b: steps(b, False), drain)

        def lagged(cur, prev, s, lag):
            b = cur if s >= lag else prev
            if b is None:
                return None
            return b, (s - lag) % PAIRS

        block = stack.enter_context(nc.Block())

        @block.sync
        def _(sp):
            sp.dma_start(x_all[:, :, :], x.rearrange("b (t p) d -> p (b t) d", p=P)).then_inc(ld_x, 16)
            sp.dma_start(wq_sb[:, :], wq).then_inc(ld_w, 16)
            sp.dma_start(wkv_sb[:, :], wkv).then_inc(ld_w, 16)
            sp.dma_start(normw_sb[:, :], norm_w.rearrange("(p a) -> p a", a=1)).then_inc(ld_c, 16)
            sp.dma_start(tab[:, :, :, :], tables).then_inc(ld_c, 16)
            sp.dma_start(wg_sb[:, :], wg).then_inc(ld_c, 16)
            sp.dma_start(ctx_b[:, :, :], ctx[0].rearrange("(t p) d -> p t d", p=P)).then_inc(ld_ctx, 16)
            sp.dma_start(wout_sb[:, :, :], wout.rearrange("(c p) d -> p c d", p=P)).then_inc(ld_wo, 16)
            sp.dma_start(fwg_sb[:, :], f_wg).then_inc(ld_wo, 16)
            sp.dma_start(bdown_sb[:, :], f_bdown).then_inc(ld_wo, 16)
            sp.dma_start(bup_rows[:, :], f_bup.rearrange("e (c p) -> (e c) p", p=P)).then_inc(ld_wo, 16)
            for e in range(2):
                sp.dma_start(wup_sb[:, e, :], f_wup[e]).then_inc(ld_e[e], 16)
                sp.dma_start(wdn_sb[:, e, :, :], f_wdown[e].rearrange("(c p) d -> p c d", p=P)).then_inc(ld_e[e], 16)
            ctx_v = ctx.rearrange("b (t p) d -> b p t d", p=P)
            with sp.Fori(0, B - 1) as i:
                sp.wait_ge(p_kv, i + 1)
                sp.dma_start(ctx_b[:, :, :], ctx_v[bass.ds(i + 1, 1)].rearrange("a p t d -> p (a t) d")).then_inc(ld_ctx, 16)
            up_v = f_wup
            dn_v = f_wdown.rearrange("e (c p) d -> e p c d", p=P)
            with sp.Fori(0, E // 2 - 1) as i:
                for e in range(2):
                    sp.wait_ge(f_dn, i * (2 * NT) + (e + 1) * NT)
                    sp.dma_start(wup_sb[:, e, :], up_v[bass.ds(i * 2 + (e + 2), 1)].rearrange("a p n -> p (a n)")).then_inc(ld_e[e], 16)
                    sp.dma_start(wdn_sb[:, e, :, :], dn_v[bass.ds(i * 2 + (e + 2), 1)].rearrange("a p c d -> p (a c) d")).then_inc(ld_e[e], 16)
            sp.wait_ge(f_sum, E * NT)
            sp.dma_start(out.rearrange("b (t p) d -> p (b t) d", p=P), x_all[:, :, :]).then_inc(stored, 16)
            sp.wait_ge(stored, 16)

        @block.gpsimd
        def _(pool):
            pool.memset(ident[:, :], 0.0).then_inc(p_chain, 1)
            pool.memset(ident16[:, :], 0.0).then_inc(p_chain, 1)
            pool.memset(mask16[:, :, :], 0.0).then_inc(p_chain, 1)
            pool.memset(tri[:, :], 1.0).then_inc(p_chain, 1)
            pool.wait_ge(p_chain, 4)
            for m in (ident, ident16):
                pool.affine_select(out=m[:, :], in_=m[:, :], compare_op=ALU.not_equal, fill=1.0, base=0,
                                   pattern=[[-1, P]], channel_multiplier=1).then_inc(consts, 1)
            pool.affine_select(out=mask16[:, :, :], in_=mask16[:, :, :], compare_op=ALU.is_ge, fill=NEG, base=0,
                               pattern=[[0, 2], [-1, P]], channel_multiplier=1).then_inc(consts, 1)
            pool.affine_select(out=tri[:, :], in_=tri[:, :], compare_op=ALU.is_ge, fill=0.0, base=0,
                               pattern=[[1, P]], channel_multiplier=-1).then_inc(consts, 1)
            pool.wait_ge(ld_c, 48)
            LINKS = 3 + 1 + 3
            BASE = 4

            def rotate(b, link0, src, dst, which):
                c, s = tab[:, 2 * which], tab[:, 2 * which + 1]

                def pairs(a):
                    return a.rearrange("p t (n two) -> p t n two", two=2)
                pool.tensor_tensor(kq1[:, :, :], src[:, :, :], c, ALU.mult).then_inc(p_chain, 1)
                for a, o in ((0, 1), (1, 0)):
                    pool.tensor_tensor(pairs(kq2[:, :, :])[:, :, :, a], pairs(src[:, :, :])[:, :, :, o],
                                       pairs(s)[:, :, :, a], ALU.mult).then_inc(p_chain, 1)
                pool.wait_ge(p_chain, at(b, LINKS, BASE + link0 + 3))
                return pool.tensor_tensor(dst[:, :, :], kq1[:, :, :], kq2[:, :, :], ALU.add)

            def outer(b):
                pool.wait_ge(ld_ctx, at(b, 16, 16))
                wait(pool, pe_RET, at(b, 4, 0))
                rotate(b, 0, ctx_b, kt, 1).then_inc(p_chain, 1)
                pool.wait_ge(p_chain, at(b, LINKS, BASE + 4))
                for t in range(T):
                    k = kt[:, t, :].rearrange("p (h d) -> p h d", h=RH)
                    v = ctx_b[:, t, :].rearrange("p (h e) -> p h e", h=RH)
                    o = kv[:, t, :, :].rearrange("p a (h d e) -> p (a h) d e", d=RD, e=RD)
                    ins = pool.tensor_tensor(o, bc(k, 3, RD), bc(v, 2, RD), ALU.mult)
                ins.then_inc(p_kv, 1)

            def queries(b):
                pool.wait_ge(v_xn2, at(b, 1, 1))
                rotate(b, 4, xn2, qt, 0).then_inc(p_q, 1)

            def keep(b):
                pool.wait_ge(v_x2, at(b, 1, 1))
                pool.tensor_copy(x_all[:, bass.ds(tile_of(b, 0), T), :], x2b[:, :, :])
                pool.wait_ge(a_xn3T, at(b, 1, 1))
                pool.tensor_copy(xn3T_all[:, bass.ds(tile_of(b, 0) * P, S)], xn3T[:, :])
                pool.wait_ge(v_cw, at(b, 1, 1))
                pool.tensor_copy(cw_all[:, bass.ds(tile_of(b, 0), T), :], cwb[:, :, :]).then_inc(p_keep, 1)

            outer(0)
            with pool.Fori(0, B - 1) as i:
                queries((i, 0))
                outer((i, 1))
                keep((i, 0))
            queries(B - 1)
            keep(B - 1)

        @block.scalar
        def _(act):
            for s in range(PAIRS):
                act.wait_ge(pw_T, s + 1)
                act.activation(wT[:, s % 2, :, :].rearrange("p a d -> p (a d)"), tb[s % 2][:, 0:2 * P], ACT.Copy).then_inc(aw_T, 1)
                act.wait_ge(pw_A, s + 1)
                for h in range(2):
                    ins = act.activation(a_sb[:, 2 * s + h, :], pair_bank[s % 2][h][:, 0:P], ACT.Copy)
                ins.then_inc(aw_A, 1)
            act.wait_ge(pw_A, PAIRS + 1)
            act.activation(bup_sb[:, :, :].rearrange("p e c -> p (e c)"), s0[:, 0:E * HC], ACT.Copy).then_inc(aw_A, 1)
            act.wait_ge(ld_c, 48)

            def xT_out(b):
                act.wait_ge(pe_XT, at(b, 1, 1))
                act.activation(xT[:, :], xb[:, S:2 * S], ACT.Copy, scale=normw_sb[:, 0:1]).then_inc(a_xT, 1)

            def z_out(b, s):
                act.wait_ge(pe_Z, at(b, PAIRS, s + 1))
                act.activation(z_sb[:, :, :].rearrange("p h j -> p (h j)"), zb[:, :], ACT.Copy).then_inc(a_z, 1)

            def probs(b, s):
                act.wait_ge(v_nm, at(b, PAIRS, s + 1))
                w = s % 2
                for h in range(2):
                    act.activation(p_sb[:, w, h, 0:P], s0[:, h * P:(h + 1) * P], ACT.Exp,
                                   bias=nmx[:, w, 0, h:h + 1], scale=SCALE)
                    ins = act.activation(p_sb[:, w, h, P:3 * P], s1[w][:, h * S:(h + 1) * S], ACT.Exp,
                                         bias=nmx[:, w, 1, h:h + 1], scale=SCALE)
                ins.then_inc(a_P, 1)

            def pT_out(b, s):
                act.wait_ge(pe_T, at(b, PAIRS, s + 1))
                act.activation(pT[:, s % 2, 1, :], tb[1][:, 0:BLOCKS * P], ACT.Copy).then_inc(a_PT, 1)

            def v_out(b, n, src, t, half):
                act.wait_ge(pe_V, at(b, 4, n))
                act.activation(v_sb[:, t, half * 8:half * 8 + 8, 0:DH], src[:, :].rearrange("p (h d) -> p h d", h=8), ACT.Copy).then_inc(a_V, 1)

            def step(cur, prev, s):
                if (w := lagged(cur, prev, s, 1)) and (cur is not None or s < 1):
                    pT_out(*w)
                if cur is not None:
                    probs(cur, s)
                    if s + 1 < PAIRS:
                        z_out(cur, s + 1)
                    if s == 0:
                        act.wait_ge(pe_G, at(cur, 1, 1))
                        act.activation(gexp[:, :, :].rearrange("p t h -> p (t h)"), xb[:, 32:32 + T * H], ACT.Exp, scale=-1.0).then_inc(a_ge, 1)
                    if s == 1:
                        v_out(cur, 1, xb, 0, 0)
                        v_out(cur, 4, tb[1], 1, 0)
                if prev is not None:
                    if s == 6:
                        act.wait_ge(pe_XN, at(prev, 1, 1))
                        wait(act, p_keep, at(prev, 1, 0))
                        act.activation(xn3T[:, :], xb[:, 0:S], ACT.Copy).then_inc(a_xn3T, 1)
                    if s == 7:
                        act.wait_ge(v_dl, at(prev, 1, 1))
                        act.activation(el[:, :, :], dl[:, :, :], ACT.Exp).then_inc(a_el, 1)

            def edge(b):
                xT_out(b)
                z_out(b, 0)

            edge(0)
            for s in range(PAIRS):
                step(0, None, s)
            edge(1)
            with act.Fori(0, B - 2) as i:
                for s in range(PAIRS):
                    step((i, 1), (i, 0), s)
                edge((i, 2))
            for s in range(PAIRS):
                step(B - 1, B - 2, s)
            for s in range(PAIRS):
                step(None, B - 1, s)
            act.wait_ge(ld_wo, 64)
            with act.Fori(0, E // 2) as i:
                for e in range(2):
                    act.activation(bup_now[:, e, :], bup_sb[:, bass.ds(i * 2 + e, 1), :].rearrange("p a c -> p (a c)"), ACT.Copy).then_inc(f_bias, 1)
                    act.wait_ge(f_bias, i * 2 + (e + 1))
                    for c in range(NT * P // CHUNK):
                        g = e * 4 + c
                        for n in range(HC):
                            act.wait_ge(f_up, i * (8 * HC) + (g * HC + n + 1))
                            act.activation(hT[:, c % 2, n, :], (s1 + tb)[n][:, :], ACT.Gelu,
                                           bias=bup_now[:, e, n:n + 1]).then_inc(f_gelu, 1)

        @block.tensor
        def _(pe):
            pe.wait_ge(consts, 4)
            pe.wait_ge(ld_w, 32)
            for s in range(PAIRS):
                if s >= 2:
                    pe.wait_ge(aw_T, s - 1)
                for q, w in ((0, wq_sb), (1, wkv_sb)):
                    ins = pe.transpose(tb[s % 2][:, q * P:(q + 1) * P], w[:, s * P:(s + 1) * P], ident[:, :])
                ins.then_inc(pw_T, 1)
                pe.wait_ge(aw_T, s + 1)
                if s >= 2:
                    pe.wait_ge(aw_A, s - 1)
                for h in range(2):
                    r = slice(h * DH, (h + 1) * DH)
                    ins = pe.matmul(pair_bank[s % 2][h][:, 0:P], wT[r, s % 2, 1, :], wT[r, s % 2, 0, :],
                                    start=True, stop=True)
                ins.then_inc(pw_A, 1)
            pe.wait_ge(aw_A, PAIRS)
            pe.wait_ge(consts_v, 3)
            pe.wait_ge(ld_c, 48)
            pe.wait_ge(ld_wo, 64)
            pe.transpose(s0[:, 0:E * HC], bup_rows[:, :], ident[0:E * HC, 0:E * HC]).then_inc(pw_A, 1)
            pe.wait_ge(aw_A, PAIRS + 1)

            def x_T(b):
                pe.wait_ge(v_xrn, at(b, 1, 1))
                if b != 0 and b != 1:
                    pe.wait_ge(v_lg, at(back(back(b)), 1, 1))
                elif b == 1:
                    pe.wait_ge(a_V, 1)
                for t in range(T):
                    ins = pe.transpose(xb[:, S + t * P:S + (t + 1) * P], xrn[:, t, :], ident[:, :])
                ins.then_inc(pe_XT, 1)

            def z_of(b, s, turned):
                wait(pe, v_oT, turned)
                if s == 0:
                    pe.wait_ge(a_xT, at(b, 1, 1))
                wait(pe, a_z, at(b, PAIRS, s))
                if s == 3:
                    pe.wait_ge(v_V, at(b, 2, 1))
                for h in range(2):
                    ins = pe.matmul(zb[:, h * S:(h + 1) * S], a_sb[:, 2 * s + h, :], xT[:, :], start=True, stop=True)
                ins.then_inc(pe_Z, 1)

            def scores(b, s):
                pe.wait_ge(a_z, at(b, PAIRS, s + 1))
                wait(pe, a_P, at(b, PAIRS, s - 1))
                w = s % 2
                zz = z_sb[:, :, :]
                s1v = s1[w][:, :].rearrange("p (h j) -> p h j", h=2)
                s0v = s0[:, 0:S].rearrange("p (h j) -> p h j", h=2)
                pe.matmul(s1v, xT[:, P:2 * P], zz, start=True, stop=False, skip_group_check=True)
                pe.matmul(s1v[:, :, P:2 * P], ident16[:, :], mask16[:, :, :], start=False, stop=True, skip_group_check=True)
                wait(pe, a_P, at(b, PAIRS, s))
                pe.matmul(s0v, xT[:, 0:P], zz[:, :, 0:P], start=True, stop=False, skip_group_check=True)
                pe.matmul(s0v, ident16[:, :], mask16[:, :, :], start=False, stop=True, skip_group_check=True).then_inc(pe_S, 1)

            def turn(b, s):
                pe.wait_ge(a_P, at(b, PAIRS, s + 1))
                wait(pe, v_PT, at(b, PAIRS, s))
                wait(pe, a_PT, at(b, PAIRS, s))
                if s == 1:
                    pe.wait_ge(v_V, at(b, 2, 2))
                    pe.wait_ge(a_V, at(b, 2, 2))
                for h in range(2):
                    for k in range(BLOCKS):
                        ins = pe.transpose(tb[h][:, k * P:(k + 1) * P], p_sb[:, s % 2, h, k * P:(k + 1) * P], ident[:, :])
                ins.then_inc(pe_T, 1)

            def weigh(b, s):
                pe.wait_ge(v_PT, at(b, PAIRS, s + 1))
                pe.wait_ge(a_PT, at(b, PAIRS, s + 1))
                wait(pe, v_norm, at(b, PAIRS, s))
                if s == 0:
                    pe.wait_ge(v_V, at(b, 2, 2))
                    pe.wait_ge(a_V, at(b, 2, 2))
                for h in range(2):
                    for qt_, blocks in ((0, (0,)), (1, (1, 2))):
                        for n, k in enumerate(blocks):
                            c = (qt_ * 2 + h) * VW
                            ins = pe.matmul(ob[:, c:c + VW], pT[:, s % 2, h, k * P:(k + 1) * P],
                                            v_sb[:, n, 2 * s + h, :], start=(n == 0), stop=(n == len(blocks) - 1))
                ins.then_inc(pe_PV, 1)

            def o_turn(b, s, z_out_of):
                pe.wait_ge(v_norm, at(b, PAIRS, s + 1))
                wait(pe, a_z, z_out_of)
                wait(pe, v_oT, at(b, PAIRS, s))
                for t in range(T):
                    ins = pe.transpose(zb[:, t * P:(t + 1) * P], o_sb[:, s % 2, t, :], ident[:, :])
                ins.then_inc(pe_OT, 1)

            def gates(b):
                for t in range(T):
                    ins = pe.matmul(xb[:, 32 + t * H:32 + (t + 1) * H], xT[:, t * P:(t + 1) * P], wg_sb[:, :], start=True, stop=True)
                ins.then_inc(pe_G, 1)

            def values(b, prev):
                pe.wait_ge(a_ge, at(b, 1, 1))
                plan = ((xb, 0, 0), (zb, 1, 1), (tb[0], 0, 1), (tb[1], 1, 0))
                for n, (dst, t, half) in enumerate(plan):
                    if n == 1:
                        pe.wait_ge(a_z, at(b, PAIRS, 3))
                        if prev is not None:
                            pe.wait_ge(v_oT, at(prev, PAIRS, 7))
                    if n == 2:
                        pe.wait_ge(v_PT, at(b, PAIRS, 1))
                        pe.wait_ge(a_PT, at(b, PAIRS, 1))
                    o = H * DH + half * 512
                    pe.matmul(dst[:, :], xT[:, t * P:(t + 1) * P], wkv_sb[:, o:o + 512], start=True, stop=True).then_inc(pe_V, 1)

            def project(b):
                pe.wait_ge(v_oT, at(b, PAIRS, PAIRS))
                for t in range(T):
                    for s in range(PAIRS):
                        ins = pe.matmul(xb[:, t * P:(t + 1) * P], oT[:, s, t, :], wout_sb[:, s, :], start=(s == 0), stop=(s == PAIRS - 1))
                ins.then_inc(pe_OUT, 1)

            def state(b, t, half):
                n = 2 * t + half
                if n == 0:
                    pe.wait_ge(v_x1, at(b, 1, 1))
                    pe.wait_ge(p_kv, at(b, 1, 1))
                else:
                    pe.wait_ge(v_ret, at(b, 4, n))
                if t:
                    pe.matmul(xb[:, :], ones[:, :], kv[:, 0, half, :], start=True, stop=False)
                pe.matmul(xb[:, :], tri[:, :], kv[:, t, half, :], start=(t == 0), stop=True).then_inc(pe_RET, 1)

            def ffn_in(b):
                pe.wait_ge(v_xn3, at(b, 1, 1))
                pe.wait_ge(v_ret, at(b, 4, 4))
                for t in range(T):
                    ins = pe.transpose(xb[:, t * P:(t + 1) * P], xn3[:, t, :], ident[:, :])
                ins.then_inc(pe_XN, 1)

            def logits(b):
                pe.wait_ge(a_xn3T, at(b, 1, 1))
                for t in range(T):
                    ins = pe.matmul(xb[:, t * E:(t + 1) * E], xn3T[:, t * P:(t + 1) * P], fwg_sb[:, :], start=True, stop=True)
                ins.then_inc(pe_LG, 1)

            def step(cur, prev, s):
                if cur is not None:
                    scores(cur, s)
                if prev is not None:
                    if s == 3:
                        project(prev)
                    if s in (4, 5):
                        state(prev, s - 4, 0)
                    if s == 7:
                        logits(prev)
                if (w := lagged(cur, prev, s, 1)) and (cur is not None or s < 1):
                    turn(*w)
                if cur is not None and s + 1 < PAIRS:
                    w4 = lagged(cur, prev, s, 4)
                    z_of(cur, s + 1, at(w4[0], PAIRS, w4[1] + 1) if w4 else 0)
                if (w := lagged(cur, prev, s, 2)) and (cur is not None or s < 2):
                    weigh(*w)
                if (w := lagged(cur, prev, s, 3)) and (cur is not None or s < 3):
                    o_turn(*w, at(prev if cur is None else cur, PAIRS, PAIRS if cur is None else min(s + 2, PAIRS)))
                if cur is not None:
                    if s == 0:
                        gates(cur)
                    if s == 1:
                        values(cur, prev)
                if prev is not None:
                    if s in (4, 5):
                        state(prev, s - 4, 1)
                    if s == 6:
                        ffn_in(prev)

            def edge(b):
                x_T(b)
                z_of(b, 0, at(back(b), PAIRS, PAIRS - 3) if b != 0 else 0)

            edge(0)
            for s in range(PAIRS):
                step(0, None, s)
            edge(1)
            with pe.Fori(0, B - 2) as i:
                for s in range(PAIRS):
                    step((i, 1), (i, 0), s)
                edge((i, 2))
            for s in range(PAIRS):
                step(B - 1, B - 2, s)
            for s in range(PAIRS):
                step(None, B - 1, s)

            pe.wait_ge(p_keep, B)
            for n in range(NT):
                if n >= 2:
                    pe.wait_ge(f_cs, n - 1)
                pe.transpose(s1[n % 2][0:E, 0:P], cw_all[:, n, :], ident[:, :]).then_inc(f_cT, 1)
                pe.wait_ge(f_cs, n + 1)
                if n >= 2:
                    pe.wait_ge(f_acc, n - 1)
                pe.matmul(tb[n % 2][:, 0:P], cwT[:, n % 2, :], bdown_sb[:, :], start=True, stop=True).then_inc(f_b, 1)
            pe.wait_ge(f_acc, NT)
            nch = NT * P // CHUNK
            ups = s1 + tb
            downs = [zb, ob]
            with pe.Fori(0, E // 2) as i:
                for e in range(2):
                    pe.wait_ge(ld_e[e], i * 32 + 32)
                    for c in range(nch):
                        g = e * nch + c

                        def up(c, g):
                            for n in range(HC):
                                if isinstance(g, int):
                                    pe.wait_ge(f_gelu, i * (2 * nch * HC) + ((g - 1) * HC + n + 1)) if g > 0 else None
                                pe.matmul(ups[n][:, :], wup_sb[:, e, n * P:(n + 1) * P],
                                          xn3T_all[:, c * CHUNK:(c + 1) * CHUNK], start=True, stop=True).then_inc(f_up, 1)
                        if g > 0:
                            up(c, g)
                        else:
                            up(c, 0)
                        pe.wait_ge(f_gelu, i * (2 * nch * HC) + (g + 1) * HC)
                        for t in range(CHUNK // P):
                            if g >= 2 and t == 0:
                                pe.wait_ge(f_sum, i * (2 * NT) + (g - 1) * (CHUNK // P))
                            for n in range(HC):
                                ins = pe.matmul(downs[c % 2][:, t * P:(t + 1) * P], hT[:, c % 2, n, t * P:(t + 1) * P],
                                                wdn_sb[:, e, n, :], start=(n == 0), stop=(n == HC - 1))
                            ins.then_inc(f_dn, 1)
                pe.wait_ge(f_sum, i * (2 * NT) + 2 * NT)

        @block.vector
        def _(dve):
            dve.memset(ones[:, :], 1.0).then_inc(consts_v, 1)
            dve.memset(v_sb[:, :, :, DH:VW], 1.0).then_inc(consts_v, 1)
            dve.memset(lg[:, :, E:LGW], NEG).then_inc(consts_v, 1)
            dve.memset(pick[:, :, TOPK:MAX8], NEG).then_inc(consts_v, 1)

            def rsqrt(link, out_, val, n):
                y, a, t = nwy[:, 0:n], nwa[:, 0:n], nwt[:, 0:n]
                link(dve.tensor_single_scalar(t.bitcast(I32), val.bitcast(I32), 1, ALU.logical_shift_right))
                link(dve.tensor_scalar(y.bitcast(I32), t.bitcast(I32), -1.0, MAGIC, ALU.mult, ALU.add))
                for k in range(4):
                    link(dve.scalar_tensor_tensor(a, y, -0.5, y, ALU.mult, ALU.mult))
                    link(dve.scalar_tensor_tensor(t, a, 1.0, val, ALU.mult, ALU.mult))
                    link(dve.scalar_tensor_tensor(y if k < 3 else out_, t, 1.5, y, ALU.add, ALU.mult))

            n1 = [0]

            def link1(ins):
                n1[0] += 1
                ins.then_inc(stat1, 1)
                dve.wait_ge(stat1, n1[0])

            dve.wait_ge(ld_x, 16)
            for n in range(NT):
                ins = dve.bn_stats(st6[:, n, :], x_all[:, n, :])
            link1(ins)
            for n in range(NT):
                ins = dve.bn_aggr(mv[:, n, :], st6[:, n, :])
            link1(ins)
            link1(dve.tensor_scalar(r_ln[:, :], mv[:, :, 1], LN_EPS, None, ALU.add))
            rsqrt(link1, r_ln[:, :], r_ln[:, :], NT)
            link1(dve.tensor_tensor(ms[:, :], r_ln[:, :], r_ln[:, :], ALU.mult))
            link1(dve.tensor_tensor(rs1[:, :], ms[:, :], mv[:, :, 1], ALU.mult))
            link1(dve.tensor_scalar(ms[:, :], rs1[:, :], RMS_EPS, None, ALU.add))
            rsqrt(link1, ms[:, :], ms[:, :], NT)
            link1(dve.tensor_tensor(rs1[:, :], ms[:, :], r_ln[:, :], ALU.mult))

            FIRST, CHAIN = 22, 71
            seen = [0]

            def chain(b):
                def link(ins, carry=False):
                    seen[0] += 1
                    ins.then_inc(v_chain, 1)
                    count = seen[0] if b == 0 else at(back(b), CHAIN, FIRST + seen[0])
                    dve.wait_ge(v_chain, count)
                    if carry:
                        dve.memset(spare[:, :], 0.0)
                return link

            def norm_in(b):
                wait(dve, pe_XT, at(b, 1, 0))
                for t in range(T):
                    n = tile_of(b, t)
                    ins = dve.tensor_scalar(xrn[:, t, :], x_all[:, bass.ds(n, 1), :].rearrange("p a d -> p (a d)"),
                                            mv[:, bass.ds(n, 1), 0], rs1[:, bass.ds(n, 1)], ALU.subtract, ALU.mult)
                ins.then_inc(v_xrn, 1)

            def maxima(b, s, link):
                dve.wait_ge(pe_S, at(b, PAIRS, s + 1))
                w = s % 2
                dve.tensor_reduce(mx[:, w, 0, :], s0[:, 0:S].rearrange("p (h j) -> p h j", h=2), AX.X, ALU.max)
                link(dve.tensor_reduce(mx[:, w, 1, :], s1[w][:, :].rearrange("p (h j) -> p h j", h=2), AX.X, ALU.max))
                dve.tensor_scalar(nmx[:, w, :, :], mx[:, w, :, :], -SCALE, None, ALU.mult).then_inc(v_nm, 1)

            def pT_out(b, s):
                dve.wait_ge(pe_T, at(b, PAIRS, s + 1))
                dve.tensor_copy(pT[:, s % 2, 0, :], tb[0][:, 0:BLOCKS * P]).then_inc(v_PT, 1)

            def normalise(b, s, link):
                if s == 0:
                    dve.wait_ge(a_ge, at(b, 1, 1))
                    link(dve.tensor_scalar(gate1[:, :, :], gexp[:, :, :], 1.0, None, ALU.add))
                    link(dve.reciprocal(gate[:, :, :], gate1[:, :, :]))
                dve.wait_ge(pe_PV, at(b, PAIRS, s + 1))
                o = ob[:, 0:4 * VW].rearrange("p (t h v) -> p t h v", t=T, h=2)
                link(dve.reciprocal(rr[:, :, :], o[:, :, :, DH]))
                link(dve.tensor_tensor(rg[:, :, :], rr[:, :, :], gate[:, :, 2 * s:2 * s + 2], ALU.mult))
                dve.tensor_tensor(o_sb[:, s % 2, :, :].rearrange("p t (h v) -> p t h v", h=2), o[:, :, :, 0:DH],
                                  bc(rg[:, :, :], 3, DH), ALU.mult).then_inc(v_norm, 1)

            def oT_out(b, s):
                dve.wait_ge(pe_OT, at(b, PAIRS, s + 1))
                dve.tensor_copy(oT[:, s, :, :].rearrange("p t i -> p (t i)"), zb[:, 0:S]).then_inc(v_oT, 1)

            def v_out(b, n, src, t, half):
                dve.wait_ge(pe_V, at(b, 4, n))
                dve.tensor_copy(v_sb[:, t, half * 8:half * 8 + 8, 0:DH], src[:, :].rearrange("p (h d) -> p h d", h=8)).then_inc(v_V, 1)

            def layernorm(link, src, dst):
                for t in range(T):
                    ins = dve.bn_stats(bst[:, t, :], src[:, t, :])
                link(ins, carry=True)
                for t in range(T):
                    ins = dve.bn_aggr(bmv[:, t, :], bst[:, t, :])
                link(ins)
                link(dve.tensor_scalar(brs[:, :], bmv[:, :, 1], LN_EPS, None, ALU.add))
                rsqrt(link, brs[:, :], brs[:, :], T)
                for t in range(T):
                    ins = dve.tensor_scalar(dst[:, t, :], src[:, t, :], bmv[:, t, 0:1], brs[:, t:t + 1], ALU.subtract, ALU.mult)
                return ins

            def first_residual(b, link):
                dve.wait_ge(pe_OUT, at(b, 1, 1))
                ins = dve.tensor_tensor(x1b[:, :, :], x_all[:, bass.ds(tile_of(b, 0), T), :],
                                        xb[:, 0:S].rearrange("p (t d) -> p t d", t=T), ALU.add)
                ins.then_inc(v_x1, 1)
                dve.wait_ge(v_x1, at(b, 1, 1))
                layernorm(link, x1b, xn2).then_inc(v_xn2, 1)

            def read_state(b, t, half, link):
                dve.wait_ge(pe_RET, at(b, 4, 2 * t + half + 1))
                if t == 0 and half == 0:
                    dve.wait_ge(p_q, at(b, 1, 1))
                q = qt[:, t, half * 64:(half + 1) * 64].rearrange("p (h d) -> p h d", h=8)
                dve.tensor_tensor(prod[:, :].rearrange("p (h e d) -> p h e d", h=8, e=RD),
                                  xb[:, :].rearrange("p (h d e) -> p h e d", h=8, d=RD),
                                  bc(q, 2, RD), ALU.mult).then_inc(v_ret, 1)
                dve.wait_ge(v_ret, at(b, 4, 2 * t + half + 1))
                link(dve.tensor_reduce(ret[:, t, half * 64:(half + 1) * 64], prod[:, :].rearrange("p (n d) -> p n d", d=RD), AX.X, ALU.add))

            def second_residual(b, link):
                wait(dve, p_keep, at(b, 1, 0))
                dve.tensor_tensor(x2b[:, :, :], x1b[:, :, :], ret[:, :, :], ALU.add).then_inc(v_x2, 1)
                dve.wait_ge(v_x2, at(b, 1, 1))
                layernorm(link, x2b, xn3).then_inc(v_xn3, 1)

            def route_a(b, link):
                dve.wait_ge(pe_LG, at(b, 1, 1))
                dve.tensor_copy(lg[:, :, 0:E], xb[:, 0:T * E].rearrange("p (t e) -> p t e", t=T)).then_inc(v_lg, 1)
                dve.wait_ge(consts_v, 4)
                dve.wait_ge(v_lg, at(b, 1, 1))
                for t in range(T):
                    ins = dve.max(top[:, t, :], lg[:, t, :])
                link(ins)
                dve.tensor_tensor(dl[:, :, :], lg[:, :, 0:E], bc(top[:, :, 0], 2, E), ALU.subtract).then_inc(v_dl, 1)
                link(dve.tensor_copy(pick[:, :, 0:TOPK], top[:, :, 0:TOPK]), carry=True)
                for t in range(T):
                    ins = dve.match_replace(rep[:, t, :], pick[:, t, :], lg[:, t, :], FOUND)
                link(ins)
                link(dve.tensor_single_scalar(hit[:, :, :], rep[:, :, 0:E], FOUND, ALU.is_equal))

            def route_b(b, link):
                dve.wait_ge(a_el, at(b, 1, 1))
                wait(dve, p_keep, at(b, 1, 0))
                link(dve.tensor_tensor(hit[:, :, :], hit[:, :, :], el[:, :, :], ALU.mult))
                link(dve.tensor_reduce(es[:, :], hit[:, :, :], AX.X, ALU.add))
                link(dve.reciprocal(er[:, :], es[:, :]))
                dve.tensor_tensor(cwb[:, :, :], hit[:, :, :], bc(er[:, :], 2, E), ALU.mult).then_inc(v_cw, 1)

            def step(cur, prev, s):
                link = chain(cur if cur is not None else prev + 1)
                if cur is not None:
                    maxima(cur, s, link)
                if prev is not None and s == 7:
                    route_a(prev, link)
                if (w := lagged(cur, prev, s, 1)) and (cur is not None or s < 1):
                    pT_out(*w)
                if (w := lagged(cur, prev, s, 2)) and (cur is not None or s < 2):
                    normalise(*w, link)
                if (w := lagged(cur, prev, s, 3)) and (cur is not None or s < 3):
                    oT_out(*w)
                if cur is not None and s == 1:
                    v_out(cur, 2, zb, 1, 1)
                    v_out(cur, 3, tb[0], 0, 1)
                if prev is not None:
                    if s == 3:
                        first_residual(prev, link)
                    if s in (4, 5):
                        read_state(prev, s - 4, 0, link)
                        read_state(prev, s - 4, 1, link)
                    if s == 5:
                        second_residual(prev, link)
                    if s == 7:
                        route_b(prev, link)

            def batch(cur, prev, nxt):
                seen[0] = 0
                for s in range(PAIRS):
                    step(cur, prev, s)
                    if s == 6 and nxt is not None:
                        norm_in(nxt)
                assert cur is None or seen[0] == (FIRST if prev is None else CHAIN), seen

            norm_in(0)
            batch(0, None, 1)
            with dve.Fori(0, B - 2) as i:
                batch((i, 1), (i, 0), (i, 2))
            batch(B - 1, B - 2, None)
            batch(None, B - 1, None)

            dve.wait_ge(p_keep, B)
            for n in range(NT):
                dve.wait_ge(f_cT, n + 1)
                if n >= 2:
                    dve.wait_ge(f_b, n - 1)
                dve.tensor_copy(cwT[:, n % 2, :], s1[n % 2][0:E, 0:P]).then_inc(f_cs, 1)
                dve.wait_ge(f_b, n + 1)
                dve.tensor_tensor(x_all[:, n, :], x_all[:, n, :], tb[n % 2][:, 0:P], ALU.add).then_inc(f_acc, 1)
            dve.wait_ge(f_acc, NT)
            with dve.Fori(0, E // 2) as i:
                for e in range(2):
                    for c in range(NT * P // CHUNK):
                        g = e * 4 + c
                        for t in range(CHUNK // P):
                            n = c * (CHUNK // P) + t
                            k = g * (CHUNK // P) + t
                            if t == 0:
                                dve.wait_ge(f_dn, i * (2 * NT) + (k + CHUNK // P))
                            if k >= NT:
                                dve.wait_ge(f_sum, i * (2 * NT) + (k + 1 - NT))
                            dve.scalar_tensor_tensor(x_all[:, n, :], (zb, ob)[c % 2][:, t * P:(t + 1) * P],
                                                     cw_all[:, n, bass.ds(i * 2 + e, 1)], x_all[:, n, :],
                                                     ALU.mult, ALU.add).then_inc(f_sum, 1)
                dve.wait_ge(f_sum, i * (2 * NT) + 2 * NT)


_INS = ['x', 'ctx_1024', 'L0_attn_norm_w', 'L0_attn_Wq', 'L0_attn_Wkv', 'L0_attn_Wout', 'L0_attn_Wg', 'L0_ffn_Wg',
        'L0_ffn_Wup', 'L0_ffn_bup', 'L0_ffn_Wdown', 'L0_ffn_bdown']


def kernel(**inputs):
    import concourse.bacc as bacc
    from concourse.bass_utils import run_bass_kernel_spmd

    nc = bacc.Bacc("TRN2", target_bir_lowering=False, num_devices=1)
    arrays, args = {}, []
    for name in _INS:
        arrays[f"in_{name}"] = np.ascontiguousarray(inputs[name])
    arrays["in_tables"] = retention_tables()
    for name, a in arrays.items():
        args.append(nc.dram_tensor(name, a.shape, mybir.dt.from_np(a.dtype), kind="ExternalInput").ap())
    args.append(nc.dram_tensor("out_0", (B, S, D), F32, kind="ExternalOutput").ap())
    decoder(nc, *args)
    r = run_bass_kernel_spmd(nc, [arrays], core_ids=[0])
    return r.results[0]["out_0"]
```

```python
from contextlib import ExitStack

import numpy as np

import concourse.bass as bass
from concourse import mybir

F32 = mybir.dt.float32
BF16 = mybir.dt.bfloat16
I32 = mybir.dt.int32
ALU = mybir.AluOpType
ACT = mybir.ActivationFunctionType
AX = mybir.AxisListType

P = 128
B, S, D = 8, 256, 128
T = S // P
NT = B * T
H, DH = 16, 64
PAIRS = H // 2
VW = DH + 1
BLOCKS = 3
RH, RD = 16, 8
HALF = RH * RD * RD // 2
E, HID, TOPK = 12, 512, 3
HC = HID // P
N = B * S
SLOTS = 256
HALVES = SLOTS // P
TILES = (N * TOPK + E * (SLOTS - 1)) // SLOTS
DEPTH = 6
GROUPS = -(-TILES // DEPTH)
TILES = GROUPS * DEPTH
CAP = N + SLOTS
PAD = S + SLOTS
ROWS = E * CAP + SLOTS
ROW = D + 1
SKIP = 1 << 20
FOUT = 4
SCALE = DH ** -0.5
NEG = -3.0e38
FOUND = 3.0e38
LN_EPS = 1e-5
RMS_EPS = float(np.finfo(np.float32).eps)
MAGIC = float(0x5F3759DF)
MAX8 = 8
LGW = E + MAX8


def retention_tables():
    half = RD // 2
    base = (np.arange(0, RD, 2, dtype=np.float32) + np.float32(0.4 * RD)) / np.float32(1.4 * RD)
    pos = np.arange(S, dtype=np.float32)
    scale = base[None, :] ** (pos / np.float32(512.0))[:, None]
    inv = np.float32(1.0) / np.float32(10000.0) ** (np.arange(half, dtype=np.float32) / np.float32(half))
    angle = pos[:, None] * inv[None, :]
    gamma = np.float32(1.0) - np.exp(np.linspace(np.log(1 / 32), np.log(1 / 512), RH)).astype(np.float32)
    decay = gamma.astype(np.float64)[None, :] ** np.arange(S)[:, None]
    sign = np.tile([-1.0, 1.0], half)
    out = []
    for s, g in ((scale, decay), (1.0 / scale, 1.0 / decay)):
        for f, w in ((np.cos(angle), np.ones(RD)), (np.sin(angle), sign)):
            t = np.repeat(f.astype(np.float64) * s, 2, axis=1) * w
            out.append((g[:, :, None] * t[:, None, :]).reshape(S, RH * RD))
    return np.stack(out).reshape(4, T, P, D).transpose(2, 0, 1, 3).astype(np.float32).copy()


def bc(ap, dim, n):
    shape = list(ap.shape)
    return ap.unsqueeze(dim).broadcast_to(shape[:dim] + [n] + shape[dim:])


def decoder(nc, x, ctx, norm_w, wq, wkv, wout, wg, f_wg, f_wup, f_bup, f_wdown, f_bdown, tables, out):
    with ExitStack() as stack:
        def sb(name, shape, dt=F32):
            return stack.enter_context(nc.sbuf_tensor(name, shape, dt))

        def bank(name):
            return stack.enter_context(nc.psum_tensor(name, [P, 512], F32))

        def sem(name):
            return stack.enter_context(nc.semaphore(name))

        x_all = sb("x_all", [P, NT, D])
        wq_sb = sb("wq_sb", [P, H * DH])
        wkv_sb = sb("wkv_sb", [P, 2 * H * DH])
        wout_sb = sb("wout_sb", [P, PAIRS, D])
        wg_sb = sb("wg_sb", [P, H])
        fwg_sb = sb("fwg_sb", [P, E])
        normw_sb = sb("normw_sb", [P, 1])
        tab = sb("tab", [P, 4, T, D])
        bup_sb = sb("bup_sb", [P, E, HC])
        bup_rows = sb("bup_rows", [E * HC, P])
        w3_all = sb("w3_all", [P, NT, TOPK])
        wT = sb("wT", [P, 2, 2, P])
        a_sb = sb("a_sb", [P, H, P])
        ident = sb("ident", [P, P])
        ident16 = sb("ident16", [P, P], BF16)
        mask16 = sb("mask16", [P, 2, P], BF16)
        tri = sb("tri", [P, P])
        ones = sb("ones", [P, P])
        st6 = sb("st6", [P, NT, 6])
        mv = sb("mv", [P, NT, 2])
        rs1 = sb("rs1", [P, NT])
        r_ln = sb("r_ln", [P, NT])
        ms = sb("ms", [P, NT])
        nwt = sb("nwt", [P, NT])
        nwa = sb("nwa", [P, NT])
        nwy = sb("nwy", [P, NT])
        xrn = sb("xrn", [P, T, D])
        xT = sb("xT", [P, S])
        gexp = sb("gexp", [P, T, H])
        gate1 = sb("gate1", [P, T, H])
        gate = sb("gate", [P, T, H])
        v_sb = sb("v_sb", [P, T, H, VW])
        z_sb = sb("z_sb", [P, 2, S])
        mx = sb("mx", [P, 2, 2, 2])
        nmx = sb("nmx", [P, 2, 2, 2])
        p_sb = sb("p_sb", [P, 2, 2, BLOCKS * P])
        pT = sb("pT", [P, 2, 2, BLOCKS * P])
        rr = sb("rr", [P, T, 2])
        rg = sb("rg", [P, T, 2])
        o_sb = sb("o_sb", [P, 2, T, P])
        oT = sb("oT", [P, PAIRS, T, P])
        x1b = sb("x1b", [P, T, D])
        x2b = sb("x2b", [P, T, D])
        bst = sb("bst", [P, T, 6])
        bmv = sb("bmv", [P, T, 2])
        brs = sb("brs", [P, T])
        brs3 = sb("brs3", [P, T])
        xn2 = sb("xn2", [P, T, D])
        xc3 = sb("xc3", [P, T, D])
        xn3 = sb("xn3", [P, T, D])
        xn3T = sb("xn3T", [P, S])
        ctx_b = sb("ctx_b", [P, T, D])
        kq1 = sb("kq1", [P, T, D])
        kq2 = sb("kq2", [P, T, D])
        kt = sb("kt", [P, T, D])
        qt = sb("qt", [P, T, D])
        kv = sb("kv", [P, T, 2, HALF])
        sum4 = sb("sum4", [P, HALF // RD, 4])
        sum2 = sb("sum2", [P, HALF // RD, 2])
        prod = sb("prod", [P, 2, HALF])
        ret = sb("ret", [P, T, D])
        lg = sb("lg", [P, T, LGW])
        top = sb("top", [P, T, MAX8])
        pick = sb("pick", [P, T, MAX8])
        rep = sb("rep", [P, T, LGW])
        hit = sb("hit", [P, T, E])
        dl = sb("dl", [P, T, E])
        el = sb("el", [P, T, E])
        es = sb("es", [P, T])
        er = sb("er", [P, T])
        hit16 = sb("hit16", [P, T, E], BF16)
        tri16 = sb("tri16", [P, P], BF16)
        ones16 = sb("ones16", [P, P], BF16)
        hw = sb("hw", [P, T, E])
        cwb = sb("cwb", [P, T, E])
        region = sb("region", [P, E])
        filled = sb("filled", [P, E])
        place = sb("place", [P, T, E])
        slot1 = sb("slot1", [P, T, E])
        last3 = sb("last3", [P, T, MAX8])
        same = sb("same", [P, T, TOPK, E])
        samew = sb("samew", [P, T, TOPK, E])
        slot_i = sb("slot_i", [P, T, TOPK], I32)
        result_row = sb("result_row", [P, T, TOPK], I32)
        packed = sb("packed", [P, T, TOPK, ROW])
        padding = sb("padding", [P, PAD // P, ROW])
        count = sb("count", [P, E])
        steps256 = sb("steps256", [P, N // SLOTS])
        more = sb("more", [P, E, N // SLOTS])
        tiles_of = sb("tiles_of", [P, E])
        upto = sb("upto", [P, E, E])
        uptot = sb("uptot", [P, E, E])
        ends = sb("ends", [P, E])
        tau = sb("tau", [P, TILES])
        past = sb("past", [P, TILES, E])
        pastn = sb("pastn", [P, TILES, E])
        eid = sb("eid", [P, TILES])
        begun = sb("begun", [P, TILES])
        off = sb("off", [P, TILES])
        row_f = sb("row_f", [P, TILES])
        plan = sb("plan", [P, 2, TILES], I32)
        pad_row = sb("pad_row", [P, E], I32)
        wup_sb = sb("wup_sb", [P, DEPTH, HID])
        wdn_sb = sb("wdn_sb", [P, DEPTH, HC, D])
        row_i = sb("row_i", [P, DEPTH, HALVES], I32)
        bup_now = sb("bup_now", [P, DEPTH, HC])
        bdn_now = sb("bdn_now", [P, DEPTH, D])
        xg = sb("xg", [P, DEPTH, HALVES, ROW])
        xgT = sb("xgT", [P, 2, SLOTS])
        hT = sb("hT", [P, 2, HC, SLOTS])
        y_sb = sb("y_sb", [P, DEPTH, HALVES, D])
        y3 = sb("y3", [P, TOPK, NT, D])
        spare = sb("spare", [P, 1])
        spare_p = sb("spare_p", [P, 4])

        s1 = [bank("s1_even"), bank("s1_odd")]
        s0 = bank("s0")
        zb = bank("zb")
        tb = [bank("tb_a"), bank("tb_b")]
        ob = bank("ob")
        xb = bank("xb")

        pair_bank = [s1, [zb, ob]]

        ld_x, ld_w, ld_wo, ld_c, ld_ctx, stored = (
            sem(n) for n in ("ld_x", "ld_w", "ld_wo", "ld_c", "ld_ctx", "stored"))
        ld_e = [sem(f"ld_e{u}") for u in range(DEPTH)]
        scattered = [sem(f"scattered{u}") for u in range(DEPTH)]
        dispatched, padded, ld_y = sem("dispatched"), sem("padded"), [sem(f"ld_y{c}") for c in range(NT // FOUT)]
        consts = sem("consts")
        consts_v = sem("consts_v")
        tables_ready = sem("tables_ready")
        pw_T, pw_A, aw_T, aw_A = sem("pw_T"), sem("pw_A"), sem("aw_T"), sem("aw_A")
        stat1 = sem("stat1")
        pe_S, pe_T, pe_PV, pe_OT, pe_Z, pe_XT, pe_G, pe_V, pe_OUT, pe_RET, pe_XN, pe_LG = (
            sem(n) for n in ("pe_S", "pe_T", "pe_PV", "pe_OT", "pe_Z", "pe_XT", "pe_G", "pe_V", "pe_OUT",
                             "pe_RET", "pe_XN", "pe_LG"))
        v_nm, v_norm, v_V, v_x1, v_x2, v_xn2, v_ret, v_xc3, v_xn3, v_lg, v_dl, v_cw, v_xrn, v_chain = (
            sem(n) for n in ("v_nm", "v_norm", "v_V", "v_x1", "v_x2", "v_xn2", "v_ret", "v_xc3", "v_xn3",
                             "v_lg", "v_dl", "v_cw", "v_xrn", "v_chain"))
        a_P, a_z, a_PT, a_oT, a_V, a_xT, a_ge, a_xn3T, a_el = (
            sem(n) for n in ("a_P", "a_z", "a_PT", "a_oT", "a_V", "a_xT", "a_ge", "a_xn3T", "a_el"))
        p_kv, p_q, p_sum, p_ret, p_pack, p_keep, p_cell, p_chain = (
            sem(n) for n in ("p_kv", "p_q", "p_sum", "p_ret", "p_pack", "p_keep", "p_cell", "p_chain"))
        pe_CNT, v_hit, v_filled, v_slot, v_pad, v_plan, v_fin = (sem(n) for n in ("pe_CNT", "v_hit", "v_filled", "v_slot", "v_pad", "v_plan", "v_fin"))
        f_T, f_xg, f_up, f_gelu, f_dn, f_y, f_out = (
            sem(n) for n in ("f_T", "f_xg", "f_up", "f_gelu", "f_dn", "f_y", "f_out"))

        xs = nc.dram_tensor("tokens_by_expert", (ROWS, ROW), F32, kind="Internal").ap()
        ys = nc.dram_tensor("results_by_token", (TOPK * N, D), F32, kind="Internal").ap()

        def at(b, per, k):
            if isinstance(b, tuple):
                return b[0] * per + (b[1] * per + k)
            return b * per + k

        def wait(eng, s, value):
            if not isinstance(value, int) or value > 0:
                eng.wait_ge(s, value)

        def back(b):
            return (b[0], b[1] - 1) if isinstance(b, tuple) else b - 1

        def after(b):
            return (b[0], b[1] + 1) if isinstance(b, tuple) else b + 1

        def tile_of(b, t):
            return (b[0] * T + (b[1] * T + t)) if isinstance(b, tuple) else b * T + t

        def lagged(cur, prev, s, lag):
            b = cur if s >= lag else prev
            if b is None:
                return None
            return b, (s - lag) % PAIRS

        block = stack.enter_context(nc.Block())

        @block.sync
        def _(sp):
            sp.dma_start(x_all[:, :, :], x.rearrange("b (t p) d -> p (b t) d", p=P)).then_inc(ld_x, 16)
            sp.dma_start(wq_sb[:, :], wq).then_inc(ld_w, 16)
            sp.dma_start(wkv_sb[:, :], wkv).then_inc(ld_w, 16)
            sp.dma_start(normw_sb[:, :], norm_w.rearrange("(p a) -> p a", a=1)).then_inc(ld_c, 16)
            sp.dma_start(tab[:, :, :, :], tables).then_inc(ld_c, 16)
            sp.dma_start(wg_sb[:, :], wg).then_inc(ld_c, 16)
            sp.dma_start(ctx_b[:, :, :], ctx[0].rearrange("(t p) d -> p t d", p=P)).then_inc(ld_ctx, 16)
            sp.dma_start(wout_sb[:, :, :], wout.rearrange("(c p) d -> p c d", p=P)).then_inc(ld_wo, 16)
            sp.dma_start(fwg_sb[:, :], f_wg).then_inc(ld_wo, 16)
            sp.dma_start(bup_rows[:, :], f_bup.rearrange("e (c p) -> (e c) p", p=P)).then_inc(ld_wo, 16)
            ctx_v = ctx.rearrange("b (t p) d -> b p t d", p=P)
            with sp.Fori(0, B - 1) as i:
                sp.wait_ge(p_kv, i + 1)
                sp.dma_start(ctx_b[:, :, :], ctx_v[bass.ds(i + 1, 1)].rearrange("a p t d -> p (a t) d")).then_inc(ld_ctx, 16)
            sp.wait_ge(v_pad, 1)
            with sp.Fori(0, E) as i:
                r = sp.value_load(pad_row[0:1, bass.ds(i, 1)], min_val=0, max_val=E * CAP - PAD)
                sp.dma_start(xs[bass.ds(r, PAD), :].rearrange("(a p) w -> p a w", p=P), padding[:, :, :]).then_inc(padded, 16)
            sp.wait_ge(v_plan, 1)

            dn_v = f_wdown.rearrange("e (c p) d -> e p c d", p=P)

            def load(g):
                for u in range(DEPTH):
                    t = (g[0] * DEPTH + (g[1] * DEPTH + u)) if isinstance(g, tuple) else g * DEPTH + u
                    wait(sp, f_y, at(back(g), DEPTH, u + 1) if g != 0 else 0)
                    r = sp.value_load(plan[0:1, 0, bass.ds(t, 1)], min_val=0, max_val=E * CAP)
                    e = sp.value_load(plan[0:1, 1, bass.ds(t, 1)], min_val=0, max_val=E - 1)
                    sp.dma_start(wup_sb[:, u, :], f_wup[bass.ds(e, 1)].rearrange("a p n -> p (a n)")).then_inc(ld_e[u], 16)
                    sp.dma_start(wdn_sb[:, u, :, :], dn_v[bass.ds(e, 1)].rearrange("a p c d -> p (a c) d")).then_inc(ld_e[u], 16)
                    sp.dma_start(bup_now[:, u, :], bup_sb[:, bass.ds(e, 1), :].rearrange("p a c -> p (a c)")).then_inc(ld_e[u], 16)
                    sp.dma_start(bdn_now[:, u, :], f_bdown[bass.ds(e, 1), :].broadcast_to([P, D])).then_inc(ld_e[u], 16)
                    if g == 0 and u == 0:
                        sp.wait_ge(dispatched, (1 + B * T * TOPK) * 16)
                    sp.dma_start(xg[:, u, :, :], xs[bass.ds(r, SLOTS), :].rearrange("(a p) w -> p a w", p=P)).then_inc(ld_e[u], 16)

            load(0)
            with sp.Fori(0, GROUPS - 1) as i:
                load((i, 1))
            for u in range(DEPTH):
                sp.wait_ge(scattered[u], GROUPS * HALVES * 16)
            y_v = ys.rearrange("(k n p) d -> p k n d", k=TOPK, p=P)
            for c in range(NT // FOUT):
                for k in range(TOPK):
                    n = slice(c * FOUT, (c + 1) * FOUT)
                    sp.dma_start(y3[:, k, n, :], y_v[:, k, n, :]).then_inc(ld_y[c], 16)
            out_v = out.rearrange("b (t p) d -> p (b t) d", p=P)
            for c in range(NT // FOUT):
                n = slice(c * FOUT, (c + 1) * FOUT)
                sp.wait_ge(f_out, c + 1)
                sp.dma_start(out_v[:, n, :], x_all[:, n, :]).then_inc(stored, 16)
            sp.wait_ge(stored, 16 * (NT // FOUT))

        @block.gpsimd
        def _(pool):
            pool.memset(ident[:, :], 0.0).then_inc(p_chain, 1)
            pool.memset(ident16[:, :], 0.0).then_inc(p_chain, 1)
            pool.memset(mask16[:, :, :], 0.0).then_inc(p_chain, 1)
            pool.memset(tri[:, :], 1.0).then_inc(p_chain, 1)
            pool.memset(tri16[:, :], 1.0).then_inc(p_chain, 1)
            pool.memset(upto[:, :, :], 1.0).then_inc(p_chain, 1)
            pool.wait_ge(p_chain, 6)
            exact = dict(allow_small_or_imprecise_dtypes=True)
            pool.iota(region[:, :], [[CAP, E]], base=0, channel_multiplier=0, **exact).then_inc(tables_ready, 1)
            pool.iota(steps256[:, :], [[SLOTS, N // SLOTS]], base=0, channel_multiplier=0, **exact).then_inc(tables_ready, 1)
            pool.iota(tau[:, :], [[1, TILES]], base=0, channel_multiplier=0, **exact).then_inc(tables_ready, 1)
            pool.iota(result_row[:, :, :], [[P, T], [N, TOPK]], base=0, channel_multiplier=1).then_inc(tables_ready, 1)
            pool.memset(padding[:, :, 0:D], 0.0).then_inc(tables_ready, 1)
            pool.iota(padding[:, :, D:ROW].bitcast(I32), [[0, PAD // P], [0, 1]], base=SKIP, channel_multiplier=0).then_inc(tables_ready, 1)
            pool.affine_select(out=upto[:, :, :], in_=upto[:, :, :], compare_op=ALU.is_ge, fill=0.0, base=0,
                               pattern=[[1, E], [-1, E]], channel_multiplier=0).then_inc(tables_ready, 1)
            for m in (ident, ident16):
                pool.affine_select(out=m[:, :], in_=m[:, :], compare_op=ALU.not_equal, fill=1.0, base=0,
                                   pattern=[[-1, P]], channel_multiplier=1).then_inc(consts, 1)
            pool.affine_select(out=mask16[:, :, :], in_=mask16[:, :, :], compare_op=ALU.is_ge, fill=NEG, base=0,
                               pattern=[[0, 2], [-1, P]], channel_multiplier=1).then_inc(consts, 1)
            for m in (tri, tri16):
                pool.affine_select(out=m[:, :], in_=m[:, :], compare_op=ALU.is_ge, fill=0.0, base=0,
                                   pattern=[[1, P]], channel_multiplier=-1).then_inc(consts, 1)
            pool.wait_ge(tables_ready, 6)
            pool.dma_start(xs[E * CAP:ROWS, :].rearrange("(a p) w -> p a w", p=P), padding[:, 0:SLOTS // P, :]).then_inc(dispatched, 16)
            pool.memset(spare_p[:, :], 0.0).then_inc(p_cell, 1)
            pool.wait_ge(ld_c, 48)
            LINKS = 3 + 1 + 3
            BASE = 6

            def rotate(b, link0, src, dst, which):
                c, s = tab[:, 2 * which], tab[:, 2 * which + 1]

                def pairs(a):
                    return a.rearrange("p t (n two) -> p t n two", two=2)
                pool.tensor_tensor(kq1[:, :, :], src[:, :, :], c, ALU.mult).then_inc(p_chain, 1)
                for a, o in ((0, 1), (1, 0)):
                    pool.tensor_tensor(pairs(kq2[:, :, :])[:, :, :, a], pairs(src[:, :, :])[:, :, :, o],
                                       pairs(s)[:, :, :, a], ALU.mult).then_inc(p_chain, 1)
                pool.wait_ge(p_chain, at(b, LINKS, BASE + link0 + 3))
                return pool.tensor_tensor(dst[:, :, :], kq1[:, :, :], kq2[:, :, :], ALU.add)

            def outer(b):
                pool.wait_ge(ld_ctx, at(b, 16, 16))
                wait(pool, pe_RET, at(b, 4, 0))
                rotate(b, 0, ctx_b, kt, 1).then_inc(p_chain, 1)
                pool.wait_ge(p_chain, at(b, LINKS, BASE + 4))
                for t in range(T):
                    k = kt[:, t, :].rearrange("p (h d) -> p h d", h=RH)
                    v = ctx_b[:, t, :].rearrange("p (h e) -> p h e", h=RH)
                    o = kv[:, t, :, :].rearrange("p a (h d e) -> p (a h) d e", d=RD, e=RD)
                    ins = pool.tensor_tensor(o, bc(k, 3, RD), bc(v, 2, RD), ALU.mult)
                ins.then_inc(p_kv, 1)

            def retained(b):
                for t in range(T):
                    for half in range(2):
                        pool.wait_ge(v_ret, at(b, 4, 2 * t + half + 1))
                        n = 2 * (2 * t + half)
                        q4, q2 = sum4[:, :, :], sum2[:, :, :]
                        pr = prod[:, half, :].rearrange("p (n d) -> p n d", d=RD)
                        pool.tensor_tensor(q4, pr[:, :, 0:4], pr[:, :, 4:8], ALU.add).then_inc(p_sum, 1)
                        pool.wait_ge(p_sum, at(b, 8, n + 1))
                        pool.tensor_tensor(q2, q4[:, :, 0:2], q4[:, :, 2:4], ALU.add).then_inc(p_sum, 1)
                        pool.wait_ge(p_sum, at(b, 8, n + 2))
                        pool.tensor_tensor(ret[:, t, half * 64:(half + 1) * 64], q2[:, :, 0], q2[:, :, 1], ALU.add).then_inc(p_ret, 1)

            def queries(b):
                pool.wait_ge(v_xn2, at(b, 1, 1))
                rotate(b, 4, xn2, qt, 0).then_inc(p_q, 1)

            def carry(n):
                return pool.tensor_tensor(spare_p[:, n:n + 1], tri[:, 0:1], tri[:, 0:1], ALU.mult)

            def pack(b):
                pool.wait_ge(v_xn3, at(b, 1, 1))
                wait(pool, dispatched, at(b, 16 * T * TOPK, 16))
                carry(0)
                for t in range(T):
                    ins = pool.tensor_copy(packed[:, t, :, 0:D], bc(xn3[:, t, :], 1, TOPK))
                ins.then_inc(p_pack, 1)

            def dispatch(b):
                if b == B - 1:
                    pool.wait_ge(padded, E * 16)
                pool.wait_ge(v_slot, at(b, 1, 1))
                pool.wait_ge(p_pack, at(b, 1, 1))
                carry(1)
                for t in range(T):
                    for k in range(TOPK):
                        pool.indirect_dma_start(
                            out=xs, out_offset=bass.IndirectOffsetOnAxis(ap=slot_i[:, t, k:k + 1], axis=0),
                            in_=packed[:, t, k, :], in_offset=None).then_inc(dispatched, 16)

            def keep(b):
                pool.wait_ge(v_x2, at(b, 1, 1))
                carry(2)
                pool.tensor_copy(x_all[:, bass.ds(tile_of(b, 0), T), :], x2b[:, :, :]).then_inc(p_keep, 1)

            outer(0)
            with pool.Fori(0, B - 1) as i:
                queries((i, 0))
                retained((i, 0))
                keep((i, 0))
                pack((i, 0))
                outer((i, 1))
                dispatch((i, 0))
            queries(B - 1)
            retained(B - 1)
            keep(B - 1)
            pack(B - 1)
            dispatch(B - 1)

            def send(g):
                for u in range(DEPTH):
                    pool.wait_ge(p_cell, at(g, DEPTH, u + 1))
                    pool.wait_ge(f_y, at(g, DEPTH, u + 1))
                    carry(3).then_inc(p_cell, 1)
                    for a in range(HALVES):
                        pool.indirect_dma_start(
                            out=ys, out_offset=bass.IndirectOffsetOnAxis(ap=row_i[:, u, a:a + 1], axis=0),
                            in_=y_sb[:, u, a, :], in_offset=None,
                            bounds_check=TOPK * N - 1, oob_is_err=False).then_inc(scattered[u], 16)

            with pool.Fori(0, GROUPS) as i:
                send((i, 0))

        @block.scalar
        def _(act):
            for s in range(PAIRS):
                act.wait_ge(pw_T, s + 1)
                act.activation(wT[:, s % 2, :, :].rearrange("p a d -> p (a d)"), tb[s % 2][:, 0:2 * P], ACT.Copy).then_inc(aw_T, 1)
                act.wait_ge(pw_A, s + 1)
                for h in range(2):
                    ins = act.activation(a_sb[:, 2 * s + h, :], pair_bank[s % 2][h][:, 0:P], ACT.Copy)
                ins.then_inc(aw_A, 1)
            act.wait_ge(pw_A, PAIRS + 1)
            act.activation(bup_sb[:, :, :].rearrange("p e c -> p (e c)"), s0[:, 0:E * HC], ACT.Copy).then_inc(aw_A, 1)
            act.wait_ge(ld_c, 48)

            def xT_out(b):
                act.wait_ge(pe_XT, at(b, 1, 1))
                act.activation(xT[:, :], zb[:, 0:S], ACT.Copy, scale=normw_sb[:, 0:1]).then_inc(a_xT, 1)

            def z_out(b, s):
                act.wait_ge(pe_Z, at(b, PAIRS, s + 1))
                act.activation(z_sb[:, :, :].rearrange("p h j -> p (h j)"), zb[:, :], ACT.Copy).then_inc(a_z, 1)

            def probs(b, s):
                act.wait_ge(v_nm, at(b, PAIRS, s + 1))
                w = s % 2
                for h in range(2):
                    act.activation(p_sb[:, w, h, 0:P], s0[:, h * P:(h + 1) * P], ACT.Exp,
                                   bias=nmx[:, w, 0, h:h + 1], scale=SCALE)
                    ins = act.activation(p_sb[:, w, h, P:3 * P], s1[w][:, h * S:(h + 1) * S], ACT.Exp,
                                         bias=nmx[:, w, 1, h:h + 1], scale=SCALE)
                ins.then_inc(a_P, 1)

            def pT_out(b, s):
                act.wait_ge(pe_T, at(b, PAIRS, s + 1))
                for h in range(2):
                    ins = act.activation(pT[:, s % 2, h, :], tb[h][:, 0:BLOCKS * P], ACT.Copy)
                ins.then_inc(a_PT, 1)

            def oT_out(b, s):
                act.wait_ge(pe_OT, at(b, PAIRS, s + 1))
                act.activation(oT[:, s, :, :].rearrange("p t i -> p (t i)"), zb[:, 0:S], ACT.Copy).then_inc(a_oT, 1)

            def v_out(b, n, src, t, half):
                act.wait_ge(pe_V, at(b, 4, n))
                act.activation(v_sb[:, t, half * 8:half * 8 + 8, 0:DH], src[:, :].rearrange("p (h d) -> p h d", h=8), ACT.Copy).then_inc(a_V, 1)

            def step(cur, prev, nxt, s):
                if cur is not None and nxt is not None and s == PAIRS - 1:
                    xT_out(nxt)
                if (w := lagged(cur, prev, s, 1)) and (cur is not None or s < 1):
                    pT_out(*w)
                if cur is not None:
                    if s + 1 < PAIRS:
                        z_out(cur, s + 1)
                    elif nxt is not None:
                        z_out(nxt, 0)
                    probs(cur, s)
                if cur is not None:
                    if s == 1:
                        act.wait_ge(pe_G, at(cur, 1, 1))
                        act.activation(gexp[:, :, :].rearrange("p t h -> p (t h)"), xb[:, 32:32 + T * H], ACT.Exp, scale=-1.0).then_inc(a_ge, 1)
                if (w := lagged(cur, prev, s, 3)) and (cur is not None or s < 3):
                    oT_out(*w)
                if cur is not None:
                    if s == 1:
                        v_out(cur, 1, xb, 0, 0)
                        v_out(cur, 4, tb[1], 1, 0)
                if prev is not None:
                    if s == 6:
                        act.wait_ge(pe_XN, at(prev, 1, 1))
                        act.activation(xn3T[:, :], xb[:, 0:S], ACT.Copy).then_inc(a_xn3T, 1)
                    if s == 7:
                        act.wait_ge(v_dl, at(prev, 1, 1))
                        act.activation(el[:, :, :], dl[:, :, :], ACT.Exp).then_inc(a_el, 1)

            xT_out(0)
            z_out(0, 0)
            for s in range(PAIRS):
                step(0, None, 1, s)
            with act.Fori(0, B - 2) as i:
                for s in range(PAIRS):
                    step((i, 1), (i, 0), (i, 2), s)
            for s in range(PAIRS):
                step(B - 1, B - 2, None, s)
            for s in range(PAIRS):
                step(None, B - 1, None, s)
            def gelu(g, u):
                for j in range(2):
                    act.wait_ge(f_up, at(g, 2 * DEPTH, 2 * u + j + 1))
                    for m in range(2):
                        n = 2 * j + m
                        ins = act.activation(hT[:, u % 2, n, :], (s1, tb)[u % 2][j][:, m * SLOTS:(m + 1) * SLOTS],
                                             ACT.Gelu, bias=bup_now[:, u, n:n + 1])
                    ins.then_inc(f_gelu, 1)

            with act.Fori(0, GROUPS) as i:
                for u in range(DEPTH):
                    gelu((i, 0), u)

        @block.tensor
        def _(pe):
            pe.wait_ge(consts, 5)
            pe.wait_ge(ld_w, 32)
            for s in range(PAIRS):
                if s >= 2:
                    pe.wait_ge(aw_T, s - 1)
                for q, w in ((0, wq_sb), (1, wkv_sb)):
                    ins = pe.transpose(tb[s % 2][:, q * P:(q + 1) * P], w[:, s * P:(s + 1) * P], ident[:, :])
                ins.then_inc(pw_T, 1)
                pe.wait_ge(aw_T, s + 1)
                if s >= 2:
                    pe.wait_ge(aw_A, s - 1)
                for h in range(2):
                    r = slice(h * DH, (h + 1) * DH)
                    ins = pe.matmul(pair_bank[s % 2][h][:, 0:P], wT[r, s % 2, 1, :], wT[r, s % 2, 0, :],
                                    start=True, stop=True)
                ins.then_inc(pw_A, 1)
            pe.wait_ge(aw_A, PAIRS)
            pe.wait_ge(consts_v, 5)
            pe.wait_ge(ld_c, 48)
            pe.wait_ge(ld_wo, 48)
            pe.transpose(s0[:, 0:E * HC], bup_rows[:, :], ident[0:E * HC, 0:E * HC]).then_inc(pw_A, 1)
            pe.wait_ge(aw_A, PAIRS + 1)

            def x_T(b):
                pe.wait_ge(v_xrn, at(b, 1, 1))
                if b != 0:
                    pe.wait_ge(a_z, at(back(b), PAIRS, PAIRS))
                    pe.wait_ge(a_oT, at(back(b), PAIRS, PAIRS - 4))
                for t in range(T):
                    ins = pe.transpose(zb[:, t * P:(t + 1) * P], xrn[:, t, :], ident[:, :])
                ins.then_inc(pe_XT, 1)

            def z_of(b, s, turned):
                wait(pe, a_oT, turned)
                if s == 0:
                    pe.wait_ge(a_xT, at(b, 1, 1))
                wait(pe, a_z, at(b, PAIRS, s))
                if s == 3:
                    pe.wait_ge(v_V, at(b, 2, 1))
                for h in range(2):
                    ins = pe.matmul(zb[:, h * S:(h + 1) * S], a_sb[:, 2 * s + h, :], xT[:, :], start=True, stop=True)
                ins.then_inc(pe_Z, 1)

            def scores(b, s):
                pe.wait_ge(a_z, at(b, PAIRS, s + 1))
                wait(pe, a_P, at(b, PAIRS, s - 1))
                w = s % 2
                zz = z_sb[:, :, :]
                s1v = s1[w][:, :].rearrange("p (h j) -> p h j", h=2)
                s0v = s0[:, 0:S].rearrange("p (h j) -> p h j", h=2)
                pe.matmul(s1v, xT[:, P:2 * P], zz, start=True, stop=False, skip_group_check=True)
                pe.matmul(s1v[:, :, P:2 * P], ident16[:, :], mask16[:, :, :], start=False, stop=True, skip_group_check=True)
                wait(pe, a_P, at(b, PAIRS, s))
                pe.matmul(s0v, xT[:, 0:P], zz[:, :, 0:P], start=True, stop=False, skip_group_check=True)
                pe.matmul(s0v, ident16[:, :], mask16[:, :, :], start=False, stop=True, skip_group_check=True).then_inc(pe_S, 1)

            def turn(b, s):
                pe.wait_ge(a_P, at(b, PAIRS, s + 1))
                wait(pe, a_PT, at(b, PAIRS, s))
                if s == 1:
                    pe.wait_ge(v_V, at(b, 2, 2))
                    pe.wait_ge(a_V, at(b, 2, 2))
                for h in range(2):
                    for k in range(BLOCKS):
                        ins = pe.transpose(tb[h][:, k * P:(k + 1) * P], p_sb[:, s % 2, h, k * P:(k + 1) * P], ident[:, :])
                ins.then_inc(pe_T, 1)

            def weigh(b, s):
                pe.wait_ge(a_PT, at(b, PAIRS, s + 1))
                wait(pe, v_norm, at(b, PAIRS, s))
                if s == 0:
                    pe.wait_ge(v_V, at(b, 2, 2))
                    pe.wait_ge(a_V, at(b, 2, 2))
                for h in range(2):
                    for qt_, blocks in ((0, (0,)), (1, (1, 2))):
                        for n, k in enumerate(blocks):
                            c = (qt_ * 2 + h) * VW
                            ins = pe.matmul(ob[:, c:c + VW], pT[:, s % 2, h, k * P:(k + 1) * P],
                                            v_sb[:, n, 2 * s + h, :], start=(n == 0), stop=(n == len(blocks) - 1))
                ins.then_inc(pe_PV, 1)

            def o_turn(b, s, z_out_of):
                pe.wait_ge(v_norm, at(b, PAIRS, s + 1))
                wait(pe, a_z, z_out_of)
                wait(pe, a_oT, at(b, PAIRS, s))
                for t in range(T):
                    ins = pe.transpose(zb[:, t * P:(t + 1) * P], o_sb[:, s % 2, t, :], ident[:, :])
                ins.then_inc(pe_OT, 1)

            def gates(b, prev):
                if prev is not None:
                    pe.wait_ge(v_nm, at(b, PAIRS, 2))
                for t in range(T):
                    ins = pe.matmul(xb[:, 32 + t * H:32 + (t + 1) * H], xT[:, t * P:(t + 1) * P], wg_sb[:, :], start=True, stop=True)
                ins.then_inc(pe_G, 1)

            def values(b, prev):
                pe.wait_ge(a_ge, at(b, 1, 1))
                plan = ((xb, 0, 0), (zb, 1, 1), (tb[0], 0, 1), (tb[1], 1, 0))
                for n, (dst, t, half) in enumerate(plan):
                    if n == 1:
                        pe.wait_ge(a_z, at(b, PAIRS, 3))
                        if prev is not None:
                            pe.wait_ge(a_oT, at(prev, PAIRS, 7))
                    if n == 2:
                        pe.wait_ge(a_PT, at(b, PAIRS, 1))
                    o = H * DH + half * 512
                    pe.matmul(dst[:, :], xT[:, t * P:(t + 1) * P], wkv_sb[:, o:o + 512], start=True, stop=True).then_inc(pe_V, 1)

            def project(cur, b, pairs):
                if cur is not None:
                    pe.wait_ge(a_V, at(cur, 2, 1))
                pe.wait_ge(a_oT, at(b, PAIRS, pairs[-1] + 1))
                for t in range(T):
                    for s in pairs:
                        ins = pe.matmul(xb[:, t * P:(t + 1) * P], oT[:, s, t, :], wout_sb[:, s, :],
                                        start=(t == 0 and s == 0), stop=(s == PAIRS - 1), skip_group_check=True)
                return ins

            def state(b, t, half):
                n = 2 * t + half
                if n == 0:
                    pe.wait_ge(v_x1, at(b, 1, 1))
                    pe.wait_ge(p_kv, at(b, 1, 1))
                else:
                    pe.wait_ge(v_ret, at(b, 4, n))
                if t:
                    pe.matmul(xb[:, :], ones[:, :], kv[:, 0, half, :], start=True, stop=False)
                pe.matmul(xb[:, :], tri[:, :], kv[:, t, half, :], start=(t == 0), stop=True).then_inc(pe_RET, 1)

            def ffn_in(b):
                pe.wait_ge(v_xc3, at(b, 1, 1))
                pe.wait_ge(v_ret, at(b, 4, 4))
                for t in range(T):
                    ins = pe.transpose(xb[:, t * P:(t + 1) * P], xc3[:, t, :], ident[:, :])
                ins.then_inc(pe_XN, 1)

            def logits(b):
                pe.wait_ge(a_xn3T, at(b, 1, 1))
                for t in range(T):
                    ins = pe.matmul(xb[:, t * E:(t + 1) * E], xn3T[:, t * P:(t + 1) * P], fwg_sb[:, :], start=True, stop=True)
                ins.then_inc(pe_LG, 1)

            def counts(b):
                pe.wait_ge(v_hit, at(b, 1, 1))
                o = [xb[:, 64 + n * E:64 + (n + 1) * E] for n in range(3)]
                pe.matmul(o[0], tri16[:, :], hit16[:, 0, :], start=True, stop=True)
                pe.matmul(o[1], ones16[:, :], hit16[:, 0, :], start=True, stop=False)
                pe.matmul(o[1], tri16[:, :], hit16[:, 1, :], start=False, stop=True)
                pe.matmul(o[2], ones16[:, :], hit16[:, 0, :], start=True, stop=False)
                pe.matmul(o[2], ones16[:, :], hit16[:, 1, :], start=False, stop=True).then_inc(pe_CNT, 1)

            def step(cur, prev, nxt, s):
                if cur is not None:
                    scores(cur, s)
                    if s == PAIRS - 1 and nxt is not None:
                        x_T(nxt)
                if prev is not None:
                    if s == 3:
                        project(cur, prev, [PAIRS - 1]).then_inc(pe_OUT, 1)
                    if s in (4, 5):
                        state(prev, s - 4, 0)
                if (w := lagged(cur, prev, s, 1)) and (cur is not None or s < 1):
                    turn(*w)
                if prev is not None and s == 2:
                    project(cur, prev, list(range(PAIRS - 1)))
                if prev is not None and s == 7:
                    logits(prev)
                if cur is not None and s == 1:
                    gates(cur, prev)
                done = at(prev, PAIRS, PAIRS + s - 3) if s < 4 and prev is not None else at(cur, PAIRS, s - 3) if cur is not None else 0
                z_seen = 0 if prev is None else at(prev, PAIRS, PAIRS)
                if cur is not None and s + 1 < PAIRS:
                    z_of(cur, s + 1, done)
                    z_seen = at(cur, PAIRS, s + 2)
                elif cur is not None:
                    z_seen = at(cur, PAIRS, PAIRS)
                    if nxt is not None:
                        z_of(nxt, 0, done)
                        z_seen = at(nxt, PAIRS, 1)
                if (w := lagged(cur, prev, s, 2)) and (cur is not None or s < 2):
                    weigh(*w)
                if (w := lagged(cur, prev, s, 3)) and (cur is not None or s < 3):
                    o_turn(*w, z_seen)
                if cur is not None:
                    if s == 1:
                        values(cur, prev)
                if prev is not None:
                    if s in (4, 5):
                        state(prev, s - 4, 1)
                    if s == 6:
                        ffn_in(prev)
                    if s == 7:
                        counts(prev)

            x_T(0)
            z_of(0, 0, 0)
            for s in range(PAIRS):
                step(0, None, 1, s)
            with pe.Fori(0, B - 2) as i:
                for s in range(PAIRS):
                    step((i, 1), (i, 0), (i, 2), s)
            for s in range(PAIRS):
                step(B - 1, B - 2, None, s)
            for s in range(PAIRS):
                step(None, B - 1, None, s)


            def turn_tokens(g, u):
                pe.wait_ge(ld_e[u], at(g, 16 * 5, 16 * 5))
                wait(pe, f_xg, at(g, DEPTH, u - 1))
                for a in range(HALVES):
                    ins = pe.transpose((xb, s0)[u % 2][:, a * P:(a + 1) * P], xg[:, u, a, 0:D], ident[:, :])
                ins.then_inc(f_T, 1)

            def up(g, u):
                pe.wait_ge(f_xg, at(g, DEPTH, u + 1))
                wait(pe, f_gelu, at(g, 2 * DEPTH, 2 * (u - 1)))
                for n in range(HC):
                    ins = pe.matmul((s1, tb)[u % 2][n // 2][:, (n % 2) * SLOTS:(n % 2 + 1) * SLOTS],
                                    wup_sb[:, u, n * P:(n + 1) * P], xgT[:, u % 2, :], start=True, stop=True)
                    if n % 2:
                        ins.then_inc(f_up, 1)

            def down(g, u):
                pe.wait_ge(f_gelu, at(g, 2 * DEPTH, 2 * (u + 1)))
                wait(pe, f_y, at(g, DEPTH, u - 1))
                for a in range(HALVES):
                    for n in range(HC):
                        ins = pe.matmul((zb, ob)[u % 2][:, a * D:(a + 1) * D], hT[:, u % 2, n, a * P:(a + 1) * P],
                                        wdn_sb[:, u, n, :], start=(n == 0), stop=(n == HC - 1))
                ins.then_inc(f_dn, 1)

            def tiles(g, first, last):
                for u in range(DEPTH):
                    if u < DEPTH - 1:
                        turn_tokens(g, u + 1)
                    elif not last:
                        turn_tokens(after(g), 0)
                    up(g, u)
                    if u:
                        down(g, u - 1)
                    elif not first:
                        down(back(g), DEPTH - 1)

            turn_tokens(0, 0)
            tiles(0, True, False)
            with pe.Fori(0, GROUPS - 2) as i:
                tiles((i, 1), False, False)
            tiles(GROUPS - 1, False, True)
            down(GROUPS - 1, DEPTH - 1)

        @block.vector
        def _(dve):
            dve.memset(ones[:, :], 1.0).then_inc(consts_v, 1)
            dve.memset(v_sb[:, :, :, DH:VW], 1.0).then_inc(consts_v, 1)
            dve.memset(lg[:, :, E:LGW], NEG).then_inc(consts_v, 1)
            dve.memset(pick[:, :, TOPK:MAX8], NEG).then_inc(consts_v, 1)
            dve.memset(ones16[:, :], 1.0).then_inc(consts_v, 1)
            dve.wait_ge(tables_ready, 7)
            dve.tensor_copy(filled[:, :], region[:, :]).then_inc(consts_v, 1)

            def rsqrt(link, out_, val, n):
                y, a, t = nwy[:, 0:n], nwa[:, 0:n], nwt[:, 0:n]
                link(dve.tensor_single_scalar(t.bitcast(I32), val.bitcast(I32), 1, ALU.logical_shift_right))
                link(dve.tensor_scalar(y.bitcast(I32), t.bitcast(I32), -1.0, MAGIC, ALU.mult, ALU.add))
                for k in range(3):
                    link(dve.scalar_tensor_tensor(a, y, -0.5, y, ALU.mult, ALU.mult))
                    link(dve.scalar_tensor_tensor(t, a, 1.0, val, ALU.mult, ALU.mult))
                    link(dve.scalar_tensor_tensor(y if k < 2 else out_, t, 1.5, y, ALU.add, ALU.mult))

            n1 = [0]

            def link1(ins):
                n1[0] += 1
                ins.then_inc(stat1, 1)
                dve.wait_ge(stat1, n1[0])

            dve.wait_ge(ld_x, 16)
            for n in range(NT):
                ins = dve.bn_stats(st6[:, n, :], x_all[:, n, :])
            link1(ins)
            for n in range(NT):
                ins = dve.bn_aggr(mv[:, n, :], st6[:, n, :])
            link1(ins)
            link1(dve.tensor_scalar(r_ln[:, :], mv[:, :, 1], LN_EPS, None, ALU.add))
            rsqrt(link1, r_ln[:, :], r_ln[:, :], NT)
            link1(dve.tensor_tensor(ms[:, :], r_ln[:, :], r_ln[:, :], ALU.mult))
            link1(dve.tensor_tensor(rs1[:, :], ms[:, :], mv[:, :, 1], ALU.mult))
            link1(dve.tensor_scalar(ms[:, :], rs1[:, :], RMS_EPS, None, ALU.add))
            rsqrt(link1, ms[:, :], ms[:, :], NT)
            link1(dve.tensor_tensor(rs1[:, :], ms[:, :], r_ln[:, :], ALU.mult))

            CHAIN = 66
            sent = [0]

            def chain(i=None):
                def link(ins, carry=False):
                    sent[0] += 1
                    ins.then_inc(v_chain, 1)
                    dve.wait_ge(v_chain, sent[0] if i is None else i * CHAIN + sent[0])
                    if carry:
                        dve.memset(spare[:, :], 0.0)
                return link

            def norm_in(b):
                wait(dve, pe_XT, at(b, 1, 0))
                for t in range(T):
                    n = tile_of(b, t)
                    ins = dve.tensor_scalar(xrn[:, t, :], x_all[:, bass.ds(n, 1), :].rearrange("p a d -> p (a d)"),
                                            mv[:, bass.ds(n, 1), 0], rs1[:, bass.ds(n, 1)], ALU.subtract, ALU.mult)
                ins.then_inc(v_xrn, 1)

            def maxima(b, s, link):
                dve.wait_ge(pe_S, at(b, PAIRS, s + 1))
                w = s % 2
                dve.tensor_reduce(mx[:, w, 0, :], s0[:, 0:S].rearrange("p (h j) -> p h j", h=2), AX.X, ALU.max)
                link(dve.tensor_reduce(mx[:, w, 1, :], s1[w][:, :].rearrange("p (h j) -> p h j", h=2), AX.X, ALU.max))
                dve.tensor_scalar(nmx[:, w, :, :], mx[:, w, :, :], -SCALE, None, ALU.mult).then_inc(v_nm, 1)

            def normalise(b, s, link):
                if s == 0:
                    dve.wait_ge(a_ge, at(b, 1, 1))
                    link(dve.tensor_scalar(gate1[:, :, :], gexp[:, :, :], 1.0, None, ALU.add))
                    link(dve.reciprocal(gate[:, :, :], gate1[:, :, :]))
                dve.wait_ge(pe_PV, at(b, PAIRS, s + 1))
                o = ob[:, 0:4 * VW].rearrange("p (t h v) -> p t h v", t=T, h=2)
                link(dve.reciprocal(rr[:, :, :], o[:, :, :, DH]))
                link(dve.tensor_tensor(rg[:, :, :], rr[:, :, :], gate[:, :, 2 * s:2 * s + 2], ALU.mult))
                dve.tensor_tensor(o_sb[:, s % 2, :, :].rearrange("p t (h v) -> p t h v", h=2), o[:, :, :, 0:DH],
                                  bc(rg[:, :, :], 3, DH), ALU.mult).then_inc(v_norm, 1)

            def v_out(b, n, src, t, half):
                dve.wait_ge(pe_V, at(b, 4, n))
                dve.tensor_copy(v_sb[:, t, half * 8:half * 8 + 8, 0:DH], src[:, :].rearrange("p (h d) -> p h d", h=8)).then_inc(v_V, 1)

            def centre(link, src, dst):
                for t in range(T):
                    ins = dve.bn_stats(bst[:, t, :], src[:, t, :])
                link(ins, carry=True)
                for t in range(T):
                    ins = dve.bn_aggr(bmv[:, t, :], bst[:, t, :])
                link(ins)
                for t in range(T):
                    ins = dve.tensor_scalar(dst[:, t, :], src[:, t, :], bmv[:, t, 0:1], None, ALU.subtract)
                return ins

            def deviation(link, dst):
                link(dve.tensor_scalar(dst[:, :], bmv[:, :, 1], LN_EPS, None, ALU.add))
                rsqrt(link, dst[:, :], dst[:, :], T)

            def first_residual(b, link):
                dve.wait_ge(pe_OUT, at(b, 1, 1))
                ins = dve.tensor_tensor(x1b[:, :, :], x_all[:, bass.ds(tile_of(b, 0), T), :],
                                        xb[:, 0:S].rearrange("p (t d) -> p t d", t=T), ALU.add)
                ins.then_inc(v_x1, 1)
                dve.wait_ge(v_x1, at(b, 1, 1))
                centre(link, x1b, xn2).then_inc(v_xn2, 1)

            def read_state(b, t, half):
                n = 2 * t + half
                dve.wait_ge(pe_RET, at(b, 4, n + 1))
                if n == 0:
                    dve.wait_ge(p_q, at(b, 1, 1))
                if n >= 2:
                    dve.wait_ge(p_ret, at(b, 4, n - 1))
                q = qt[:, t, half * 64:(half + 1) * 64].rearrange("p (h d) -> p h d", h=8)
                dve.tensor_tensor(prod[:, half, :].rearrange("p (h e d) -> p h e d", h=8, e=RD),
                                  xb[:, :].rearrange("p (h d e) -> p h e d", h=8, d=RD),
                                  bc(q, 2, RD), ALU.mult).then_inc(v_ret, 1)

            def second_residual(b, link):
                dve.wait_ge(p_ret, at(b, 4, 4))
                for t in range(T):
                    ins = dve.scalar_tensor_tensor(x2b[:, t, :], ret[:, t, :], brs[:, t:t + 1], x1b[:, t, :], ALU.mult, ALU.add)
                ins.then_inc(v_x2, 1)
                dve.wait_ge(v_x2, at(b, 1, 1))
                centre(link, x2b, xc3).then_inc(v_xc3, 1)

            def scale_third(link):
                deviation(link, brs3)
                for t in range(T):
                    ins = dve.tensor_scalar(xn3[:, t, :], xc3[:, t, :], brs3[:, t:t + 1], None, ALU.mult)
                ins.then_inc(v_xn3, 1)

            def route_a(b, link):
                dve.wait_ge(pe_LG, at(b, 1, 1))
                dve.tensor_tensor(lg[:, :, 0:E], xb[:, 0:T * E].rearrange("p (t e) -> p t e", t=T),
                                  bc(brs3[:, :], 2, E), ALU.mult).then_inc(v_lg, 1)
                dve.wait_ge(consts_v, 4)
                dve.wait_ge(v_lg, at(b, 1, 1))
                for t in range(T):
                    ins = dve.max(top[:, t, :], lg[:, t, :])
                link(ins)
                dve.tensor_tensor(dl[:, :, :], lg[:, :, 0:E], bc(top[:, :, 0], 2, E), ALU.subtract).then_inc(v_dl, 1)
                link(dve.tensor_copy(pick[:, :, 0:TOPK], top[:, :, 0:TOPK]), carry=True)
                for t in range(T):
                    ins = dve.match_replace(rep[:, t, :], pick[:, t, :], lg[:, t, :], FOUND)
                link(ins)
                dve.tensor_single_scalar(hit16[:, :, :], rep[:, :, 0:E], FOUND, ALU.is_equal).then_inc(v_hit, 1)
                link(dve.tensor_single_scalar(hit[:, :, :], rep[:, :, 0:E], FOUND, ALU.is_equal))

            def route_b(b, link):
                dve.wait_ge(a_el, at(b, 1, 1))
                link(dve.tensor_tensor(hw[:, :, :], hit[:, :, :], el[:, :, :], ALU.mult))
                link(dve.tensor_reduce(es[:, :], hw[:, :, :], AX.X, ALU.add))
                link(dve.reciprocal(er[:, :], es[:, :]))
                dve.tensor_tensor(cwb[:, :, :], hw[:, :, :], bc(er[:, :], 2, E), ALU.mult)
                dve.wait_ge(pe_CNT, at(b, 1, 1))
                link(dve.tensor_tensor(place[:, :, :], xb[:, 64:64 + T * E].rearrange("p (t e) -> p t e", t=T),
                                       bc(filled[:, :], 1, T), ALU.add))
                dve.tensor_tensor(slot1[:, :, :], place[:, :, :], hit[:, :, :], ALU.mult)
                dve.tensor_tensor(filled[:, :], filled[:, :], xb[:, 64 + T * E:64 + 3 * E], ALU.add).then_inc(v_filled, 1)

            def route_c(b, link):
                dve.wait_ge(v_filled, at(b, 1, 1))
                dve.memset(spare[:, :], 0.0)
                for t in range(T):
                    ins = dve.max(last3[:, t, :], slot1[:, t, :])
                wait(dve, dispatched, at(b, 16 * T * TOPK, 16))
                link(ins)
                dve.tensor_scalar(slot_i[:, :, :], last3[:, :, 0:TOPK], -1.0, None, ALU.add)
                link(dve.tensor_tensor(same[:, :, :, :], bc(slot1[:, :, :], 2, TOPK), bc(last3[:, :, 0:TOPK], 3, E), ALU.is_equal))
                dve.tensor_copy(packed[:, :, :, D].bitcast(I32), result_row[:, :, :]).then_inc(v_slot, 1)
                link(dve.tensor_tensor(samew[:, :, :, :], same[:, :, :, :], bc(cwb[:, :, :], 2, TOPK), ALU.mult))
                dve.tensor_scalar(result_row[:, :, :], result_row[:, :, :], float(S), None, ALU.add)
                link(dve.tensor_reduce(w3_all[:, bass.ds(tile_of(b, 0), T), :], samew[:, :, :, :], AX.X, ALU.add))

            def step(cur, prev, older, s, link):
                if cur is not None:
                    maxima(cur, s, link)
                if older is not None and s == 0:
                    route_b(older, link)
                if prev is not None:
                    if s == 4:
                        deviation(link, brs)
                    if s in (4, 5):
                        read_state(prev, s - 4, 0)
                    if s == 6:
                        second_residual(prev, link)
                    if s == 7:
                        route_a(prev, link)
                if (cur is not None or prev is not None) and (w := lagged(cur, prev, s, 2)) and (cur is not None or s < 2):
                    normalise(*w, link)
                if cur is not None and s == 1:
                    v_out(cur, 2, zb, 1, 1)
                    v_out(cur, 3, tb[0], 0, 1)
                if prev is not None:
                    if s == 3:
                        first_residual(prev, link)
                    if s in (4, 5):
                        read_state(prev, s - 4, 1)
                    if s == 6:
                        scale_third(link)
                if older is not None and s == 1:
                    route_c(older, link)

            def batch(cur, prev, nxt, link):
                for s in range(2, PAIRS):
                    step(cur, prev, None, s, link)
                    if s == 2 and nxt is not None:
                        norm_in(nxt)
                for s in range(2):
                    step(nxt, cur, prev, s, link)

            norm_in(0)
            step(0, None, None, 0, chain())
            step(0, None, None, 1, chain())
            batch(0, None, 1, chain())
            with dve.Fori(0, B - 2) as i:
                before = sent[0]
                batch((i, 1), (i, 0), (i, 2), chain(i))
                assert sent[0] - before == CHAIN, sent[0] - before
            sent[0] += (B - 3) * CHAIN
            batch(B - 1, B - 2, None, chain())
            dve.wait_ge(v_filled, B - 1)
            dve.tensor_copy(pad_row[:, :], filled[:, :]).then_inc(v_pad, 1)
            batch(None, B - 1, None, chain())

            fin = [0]

            def linkp(ins):
                fin[0] += 1
                ins.then_inc(v_fin, 1)
                dve.wait_ge(v_fin, fin[0])

            linkp(dve.tensor_tensor(count[:, :], filled[:, :], region[:, :], ALU.subtract))
            M = N // SLOTS
            linkp(dve.tensor_tensor(more[:, :, :], bc(count[:, :], 2, M), bc(steps256[:, :], 1, E), ALU.is_gt))
            linkp(dve.tensor_reduce(tiles_of[:, :], more[:, :, :], AX.X, ALU.add))
            linkp(dve.tensor_tensor(uptot[:, :, :], upto[:, :, :], bc(tiles_of[:, :], 1, E), ALU.mult))
            linkp(dve.tensor_reduce(ends[:, :], uptot[:, :, :], AX.X, ALU.add))
            linkp(dve.tensor_tensor(past[:, :, :], bc(ends[:, :], 1, TILES), bc(tau[:, :], 2, E), ALU.is_le))
            linkp(dve.tensor_tensor(pastn[:, :, :], past[:, :, :], bc(ends[:, :], 1, TILES), ALU.mult))
            dve.tensor_reduce(eid[:, :], past[:, :, :], AX.X, ALU.add)
            linkp(dve.tensor_reduce(begun[:, :], pastn[:, :, :], AX.X, ALU.max))
            dve.tensor_scalar(plan[:, 1, :], eid[:, :], float(E - 1), None, ALU.min)
            linkp(dve.tensor_tensor(off[:, :], tau[:, :], begun[:, :], ALU.subtract))
            linkp(dve.tensor_scalar(off[:, :], off[:, :], float(SLOTS), None, ALU.mult))
            linkp(dve.scalar_tensor_tensor(row_f[:, :], eid[:, :], float(CAP), off[:, :], ALU.mult, ALU.add))
            dve.tensor_scalar(plan[:, 0, :], row_f[:, :], float(E * CAP), None, ALU.min).then_inc(v_plan, 1)


            def tokens(g, u):
                dve.wait_ge(f_T, at(g, DEPTH, u + 1))
                dve.tensor_copy(xgT[:, u % 2, :], (xb, s0)[u % 2][:, 0:SLOTS]).then_inc(f_xg, 1)
                if g != 0:
                    dve.wait_ge(scattered[u], at(g, 16 * HALVES, 0))
                dve.tensor_copy(row_i[:, u, :], xg[:, u, :, D].bitcast(I32))

            def results(g, u):
                dve.wait_ge(f_dn, at(g, DEPTH, u + 1))
                dve.tensor_tensor(y_sb[:, u, :, :], (zb, ob)[u % 2][:, 0:HALVES * D].rearrange("p (a d) -> p a d", a=HALVES),
                                  bc(bdn_now[:, u, :], 1, HALVES), ALU.add).then_inc(f_y, 1)

            def tiles(g, first, last):
                for u in range(DEPTH):
                    if u < DEPTH - 1:
                        tokens(g, u + 1)
                    elif not last:
                        tokens(after(g), 0)
                    if u:
                        results(g, u - 1)
                    elif not first:
                        results(back(g), DEPTH - 1)

            tokens(0, 0)
            tiles(0, True, False)
            with dve.Fori(0, GROUPS - 2) as i:
                tiles((i, 1), False, False)
            tiles(GROUPS - 1, False, True)
            results(GROUPS - 1, DEPTH - 1)

            dve.wait_ge(p_keep, B)
            for c in range(NT // FOUT):
                dve.wait_ge(ld_y[c], 16 * TOPK)
                for k in range(TOPK):
                    for n in range(c * FOUT, (c + 1) * FOUT):
                        ins = dve.scalar_tensor_tensor(x_all[:, n, :], y3[:, k, n, :], w3_all[:, n, k:k + 1], x_all[:, n, :],
                                                       ALU.mult, ALU.add)
                    if k < TOPK - 1:
                        linkp(ins)
                ins.then_inc(f_out, 1)


_INS = ['x', 'ctx_1024', 'L0_attn_norm_w', 'L0_attn_Wq', 'L0_attn_Wkv', 'L0_attn_Wout', 'L0_attn_Wg', 'L0_ffn_Wg',
        'L0_ffn_Wup', 'L0_ffn_bup', 'L0_ffn_Wdown', 'L0_ffn_bdown']


def kernel(**inputs):
    import concourse.bacc as bacc
    from concourse.bass_utils import run_bass_kernel_spmd

    nc = bacc.Bacc("TRN2", target_bir_lowering=False, num_devices=1)
    arrays, args = {}, []
    for name in _INS:
        arrays[f"in_{name}"] = np.ascontiguousarray(inputs[name])
    arrays["in_tables"] = retention_tables()
    for name, a in arrays.items():
        args.append(nc.dram_tensor(name, a.shape, mybir.dt.from_np(a.dtype), kind="ExternalInput").ap())
    args.append(nc.dram_tensor("out_0", (B, S, D), F32, kind="ExternalOutput").ap())
    decoder(nc, *args)
    r = run_bass_kernel_spmd(nc, [arrays], core_ids=[0])
    return r.results[0]["out_0"]
```

```python
from contextlib import ExitStack

import numpy as np

import concourse.bass as bass
from concourse import mybir

F32 = mybir.dt.float32
F32R = mybir.dt.float32r
BF16 = mybir.dt.bfloat16
I32 = mybir.dt.int32
ALU = mybir.AluOpType
ACT = mybir.ActivationFunctionType
AX = mybir.AxisListType

P = 128
B, S, D = 8, 256, 128
T = S // P
NT = B * T
H, DH = 16, 64
PAIRS = H // 2
VW = DH + 1
BLOCKS = 3
RH, RD = 16, 8
HALF = RH * RD * RD // 2
E, HID, TOPK = 12, 512, 3
HC = HID // P
N = B * S
SLOTS = 256
HALVES = SLOTS // P
TILES = (N * TOPK + E * (SLOTS - 1)) // SLOTS
DEPTH = 6
AHEAD = 4
GROUPS = -(-TILES // DEPTH)
TILES = GROUPS * DEPTH
CAP = N + SLOTS
PAD = S + SLOTS
ROWS = E * CAP + SLOTS
ROW = D + 1
SKIP = 1 << 20
FOUT = 4
SCALE = DH ** -0.5
NEG = -3.0e38
FOUND = 3.0e38
LN_EPS = 1e-5
RMS_EPS = float(np.finfo(np.float32).eps)
MAGIC = float(0x5F3759DF)
MAX8 = 8
LGW = E + MAX8


def retention_tables():
    half = RD // 2
    base = (np.arange(0, RD, 2, dtype=np.float32) + np.float32(0.4 * RD)) / np.float32(1.4 * RD)
    pos = np.arange(S, dtype=np.float32)
    scale = base[None, :] ** (pos / np.float32(512.0))[:, None]
    inv = np.float32(1.0) / np.float32(10000.0) ** (np.arange(half, dtype=np.float32) / np.float32(half))
    angle = pos[:, None] * inv[None, :]
    gamma = np.float32(1.0) - np.exp(np.linspace(np.log(1 / 32), np.log(1 / 512), RH)).astype(np.float32)
    decay = gamma.astype(np.float64)[None, :] ** np.arange(S)[:, None]
    sign = np.tile([-1.0, 1.0], half)
    out = []
    for s, g in ((scale, decay), (1.0 / scale, 1.0 / decay)):
        for f, w in ((np.cos(angle), np.ones(RD)), (np.sin(angle), sign)):
            t = np.repeat(f.astype(np.float64) * s, 2, axis=1) * w
            out.append((g[:, :, None] * t[:, None, :]).reshape(S, RH * RD))
    return np.stack(out).reshape(4, T, P, D).transpose(2, 0, 1, 3).astype(np.float32).copy()


def bc(ap, dim, n):
    shape = list(ap.shape)
    return ap.unsqueeze(dim).broadcast_to(shape[:dim] + [n] + shape[dim:])


def decoder(nc, x, ctx, norm_w, wq, wkv, wout, wg, f_wg, f_wup, f_bup, f_wdown, f_bdown, tables, out):
    with ExitStack() as stack:
        def sb(name, shape, dt=F32):
            return stack.enter_context(nc.sbuf_tensor(name, shape, dt))

        def bank(name):
            return stack.enter_context(nc.psum_tensor(name, [P, 512], F32))

        def sem(name):
            return stack.enter_context(nc.semaphore(name))

        x_all = sb("x_all", [P, NT, D])
        wq_sb = sb("wq_sb", [P, H * DH])
        wkv_sb = sb("wkv_sb", [P, 2 * H * DH])
        wout_sb = sb("wout_sb", [P, PAIRS, D])
        wg_sb = sb("wg_sb", [P, H])
        fwg_sb = sb("fwg_sb", [P, E])
        normw_sb = sb("normw_sb", [P, 1])
        tab = sb("tab", [P, 4, T, D])
        bup_sb = sb("bup_sb", [P, E, HC])
        bup_rows = sb("bup_rows", [E * HC, P])
        w3_all = sb("w3_all", [P, NT, TOPK])
        wT = sb("wT", [P, 2, 2, P])
        a_sb = sb("a_sb", [P, H, P])
        a_hi = sb("a_hi", [P, H, P], F32R)
        a_lo = sb("a_lo", [P, H, P], F32R)
        wv_hi = sb("wv_hi", [P, H * DH], F32R)
        wv_lo = sb("wv_lo", [P, H * DH], F32R)
        xT_hi = sb("xT_hi", [P, S], F32R)
        xT_lo = sb("xT_lo", [P, S], F32R)
        xN = sb("xN", [P, S])
        xN_hi = sb("xN_hi", [P, S], F32R)
        xN_lo = sb("xN_lo", [P, S], F32R)
        z_hi = sb("z_hi", [P, 2, S], F32R)
        z_lo = sb("z_lo", [P, 2, S], F32R)
        ident = sb("ident", [P, P])
        ident16 = sb("ident16", [P, P], BF16)
        mask16 = sb("mask16", [P, 2, P], BF16)
        tri = sb("tri", [P, P])
        ones = sb("ones", [P, P])
        st6 = sb("st6", [P, NT, 6])
        mv = sb("mv", [P, NT, 2])
        rs1 = sb("rs1", [P, NT])
        r_ln = sb("r_ln", [P, NT])
        ms = sb("ms", [P, NT])
        nwt = sb("nwt", [P, NT])
        nwa = sb("nwa", [P, NT])
        nwy = sb("nwy", [P, NT])
        xrn = sb("xrn", [P, T, D])
        gexp = sb("gexp", [P, T, H])
        gate1 = sb("gate1", [P, T, H])
        gate = sb("gate", [P, T, H])
        v_sb = sb("v_sb", [P, T, H, VW])
        mx = sb("mx", [P, 2, 2, 2])
        nmx = sb("nmx", [P, 2, 2, 2])
        p_sb = sb("p_sb", [P, 2, 2, BLOCKS * P])
        pT = sb("pT", [P, 2, 2, BLOCKS * P])
        rr = sb("rr", [P, T, 2])
        rg = sb("rg", [P, T, 2])
        o_sb = sb("o_sb", [P, 2, T, P])
        oT = sb("oT", [P, PAIRS, T, P])
        x1b = sb("x1b", [P, T, D])
        x2b = sb("x2b", [P, T, D])
        bst = sb("bst", [P, T, 6])
        bmv = sb("bmv", [P, T, 2])
        brs = sb("brs", [P, T])
        brs3 = sb("brs3", [P, T])
        xn2 = sb("xn2", [P, T, D])
        xc3 = sb("xc3", [P, T, D])
        xn3 = sb("xn3", [P, T, D])
        xn3T = sb("xn3T", [P, S])
        ctx_b = sb("ctx_b", [P, T, D])
        kq1 = sb("kq1", [P, T, D])
        kq2 = sb("kq2", [P, T, D])
        kt = sb("kt", [P, T, D])
        qt = sb("qt", [P, T, D])
        kv = sb("kv", [P, T, 2, HALF])
        sum4 = sb("sum4", [P, HALF // RD, 4])
        sum2 = sb("sum2", [P, HALF // RD, 2])
        prod = sb("prod", [P, 2, HALF])
        ret = sb("ret", [P, T, D])
        lg = sb("lg", [P, T, LGW])
        top = sb("top", [P, T, MAX8])
        pick = sb("pick", [P, T, MAX8])
        rep = sb("rep", [P, T, LGW])
        hit = sb("hit", [P, T, E])
        dl = sb("dl", [P, T, E])
        el = sb("el", [P, T, E])
        es = sb("es", [P, T])
        er = sb("er", [P, T])
        hit16 = sb("hit16", [P, T, E], BF16)
        tri16 = sb("tri16", [P, P], BF16)
        ones16 = sb("ones16", [P, P], BF16)
        hw = sb("hw", [P, T, E])
        cwb = sb("cwb", [P, T, E])
        region = sb("region", [P, E])
        filled = sb("filled", [P, E])
        place = sb("place", [P, T, E])
        slot1 = sb("slot1", [P, T, E])
        last3 = sb("last3", [P, T, MAX8])
        same = sb("same", [P, T, TOPK, E])
        samew = sb("samew", [P, T, TOPK, E])
        slot_i = sb("slot_i", [P, T, TOPK], I32)
        result_row = sb("result_row", [P, T, TOPK], I32)
        packed = sb("packed", [P, T, TOPK, ROW])
        padding = sb("padding", [P, PAD // P, ROW])
        count = sb("count", [P, E])
        steps256 = sb("steps256", [P, N // SLOTS])
        more = sb("more", [P, E, N // SLOTS])
        tiles_of = sb("tiles_of", [P, E])
        upto = sb("upto", [P, E, E])
        uptot = sb("uptot", [P, E, E])
        ends = sb("ends", [P, E])
        tau = sb("tau", [P, TILES])
        past = sb("past", [P, TILES, E])
        pastn = sb("pastn", [P, TILES, E])
        eid = sb("eid", [P, TILES])
        begun = sb("begun", [P, TILES])
        off = sb("off", [P, TILES])
        row_f = sb("row_f", [P, TILES])
        plan = sb("plan", [P, 2, TILES], I32)
        pad_row = sb("pad_row", [P, E], I32)
        wup_sb = sb("wup_sb", [P, DEPTH, HID])
        wdn_sb = sb("wdn_sb", [P, DEPTH, HC, D])
        row_i = sb("row_i", [P, DEPTH, HALVES], I32)
        bup_now = sb("bup_now", [P, DEPTH, HC])
        bdn_now = sb("bdn_now", [P, DEPTH, D])
        xg = sb("xg", [P, DEPTH, HALVES, ROW])
        wup_hi = sb("wup_hi", [P, 2, HID], F32R)
        wup_lo = sb("wup_lo", [P, 2, HID], F32R)
        xgT_hi = sb("xgT_hi", [P, 2, SLOTS], F32R)
        xgT_lo = sb("xgT_lo", [P, 2, SLOTS], F32R)
        hT = sb("hT", [P, 2, HC, SLOTS])
        y_sb = sb("y_sb", [P, DEPTH, HALVES, D])
        y3 = [a[:, 0:TOPK * FOUT * D].rearrange("p (k n d) -> p k n d", k=TOPK, n=FOUT) for a in (
            wkv_sb, a_sb[:, :, :].rearrange("p h d -> p (h d)"),
            p_sb[:, :, :, :].rearrange("p a h k -> p (a h k)"), pT[:, :, :, :].rearrange("p a h k -> p (a h k)"))]
        spare = sb("spare", [P, 1])
        spare_p = sb("spare_p", [P, 4])

        s1 = [bank("s1_even"), bank("s1_odd")]
        s0 = bank("s0")
        zb = bank("zb")
        tb = [bank("tb_a"), bank("tb_b")]
        ob = bank("ob")
        xb = bank("xb")

        pair_bank = [s1, [zb, ob]]

        ld_x, ld_w, ld_wo, ld_c, ld_ctx, stored = (
            sem(n) for n in ("ld_x", "ld_w", "ld_wo", "ld_c", "ld_ctx", "stored"))
        ld_e = [sem(f"ld_e{u}") for u in range(DEPTH)]
        ld_b = [sem(f"ld_b{u}") for u in range(DEPTH)]
        scattered = [sem(f"scattered{u}") for u in range(DEPTH)]
        dispatched, padded, ld_y = sem("dispatched"), sem("padded"), [sem(f"ld_y{c}") for c in range(NT // FOUT)]
        consts = sem("consts")
        consts_v = sem("consts_v")
        tables_ready = sem("tables_ready")
        pw_T, pw_A, aw_T, aw_A = sem("pw_T"), sem("pw_A"), sem("aw_T"), sem("aw_A")
        stat1 = sem("stat1")
        pe_S, pe_T, pe_PV, pe_OT, pe_Z, pe_XT, pe_G, pe_V, pe_OUT, pe_RET, pe_XN, pe_LG = (
            sem(n) for n in ("pe_S", "pe_T", "pe_PV", "pe_OT", "pe_Z", "pe_XT", "pe_G", "pe_V", "pe_OUT",
                             "pe_RET", "pe_XN", "pe_LG"))
        v_nm, v_split, v_xlo, v_z, v_norm, v_V, v_x1, v_x2, v_xn2, v_ret, v_xc3, v_xn3, v_lg, v_dl, v_xrn, v_chain = (
            sem(n) for n in ("v_nm", "v_split", "v_xlo", "v_z", "v_norm", "v_V", "v_x1", "v_x2", "v_xn2", "v_ret", "v_xc3", "v_xn3",
                             "v_lg", "v_dl", "v_xrn", "v_chain"))
        a_P, a_z, a_hi_wv, a_PT, a_oT, a_V, a_xT, a_xN, a_ge, a_xn3T, a_el = (
            sem(n) for n in ("a_P", "a_z", "a_hi_wv", "a_PT", "a_oT", "a_V", "a_xT", "a_xN", "a_ge", "a_xn3T", "a_el"))
        p_kv, p_q, p_sum, p_ret, p_pack, p_keep, p_cell, p_chain = (
            sem(n) for n in ("p_kv", "p_q", "p_sum", "p_ret", "p_pack", "p_keep", "p_cell", "p_chain"))
        pe_CNT, v_hit, v_filled, v_slot, v_pad, v_plan, v_fin = (sem(n) for n in ("pe_CNT", "v_hit", "v_filled", "v_slot", "v_pad", "v_plan", "v_fin"))
        f_T, f_hi, f_w, f_xg, f_up, f_gelu, f_dn, f_y, f_out = (
            sem(n) for n in ("f_T", "f_hi", "f_w", "f_xg", "f_up", "f_gelu", "f_dn", "f_y", "f_out"))

        xs = nc.dram_tensor("tokens_by_expert", (ROWS, ROW), F32, kind="Internal").ap()
        ys = nc.dram_tensor("results_by_token", (TOPK * N, D), F32, kind="Internal").ap()

        def at(b, per, k):
            if isinstance(b, tuple):
                return b[0] * per + (b[1] * per + k)
            return b * per + k

        def wait(eng, s, value):
            if not isinstance(value, int) or value > 0:
                eng.wait_ge(s, value)

        def back(b):
            return (b[0], b[1] - 1) if isinstance(b, tuple) else b - 1

        def after(b):
            return (b[0], b[1] + 1) if isinstance(b, tuple) else b + 1

        def tile_of(b, t):
            return (b[0] * T + (b[1] * T + t)) if isinstance(b, tuple) else b * T + t

        def lagged(cur, prev, s, lag):
            b = cur if s >= lag else prev
            if b is None:
                return None
            return b, (s - lag) % PAIRS

        block = stack.enter_context(nc.Block())

        @block.sync
        def _(sp):
            sp.dma_start(wq_sb[:, :], wq).then_inc(ld_w, 16)
            sp.dma_start(wkv_sb[:, :], wkv).then_inc(ld_w, 16)
            sp.dma_start(x_all[:, :, :], x.rearrange("b (t p) d -> p (b t) d", p=P)).then_inc(ld_x, 16)
            sp.dma_start(normw_sb[:, :], norm_w.rearrange("(p a) -> p a", a=1)).then_inc(ld_c, 16)
            sp.dma_start(tab[:, :, :, :], tables).then_inc(ld_c, 16)
            sp.dma_start(wg_sb[:, :], wg).then_inc(ld_c, 16)
            sp.dma_start(ctx_b[:, :, :], ctx[0].rearrange("(t p) d -> p t d", p=P)).then_inc(ld_ctx, 16)
            sp.dma_start(wout_sb[:, :, :], wout.rearrange("(c p) d -> p c d", p=P)).then_inc(ld_wo, 16)
            sp.dma_start(fwg_sb[:, :], f_wg).then_inc(ld_wo, 16)
            sp.dma_start(bup_rows[:, :], f_bup.rearrange("e (c p) -> (e c) p", p=P)).then_inc(ld_wo, 16)
            ctx_v = ctx.rearrange("b (t p) d -> b p t d", p=P)
            with sp.Fori(0, B - 1) as i:
                sp.wait_ge(p_kv, i + 1)
                sp.dma_start(ctx_b[:, :, :], ctx_v[bass.ds(i + 1, 1)].rearrange("a p t d -> p (a t) d")).then_inc(ld_ctx, 16)
            sp.wait_ge(v_pad, 1)
            with sp.Fori(0, E) as i:
                r = sp.value_load(pad_row[0:1, bass.ds(i, 1)], min_val=0, max_val=E * CAP - PAD)
                sp.dma_start(xs[bass.ds(r, PAD), :].rearrange("(a p) w -> p a w", p=P), padding[:, :, :]).then_inc(padded, 16)
            sp.wait_ge(v_plan, 1)

            dn_v = f_wdown.rearrange("e (c p) d -> e p c d", p=P)

            def load(g):
                for u in range(DEPTH):
                    t = (g[0] * DEPTH + (g[1] * DEPTH + u)) if isinstance(g, tuple) else g * DEPTH + u
                    wait(sp, f_y, at(back(g), DEPTH, u + 1) if g != 0 else 0)
                    r = sp.value_load(plan[0:1, 0, bass.ds(t, 1)], min_val=0, max_val=E * CAP)
                    e = sp.value_load(plan[0:1, 1, bass.ds(t, 1)], min_val=0, max_val=E - 1)
                    sp.dma_start(wup_sb[:, u, :], f_wup[bass.ds(e, 1)].rearrange("a p n -> p (a n)")).then_inc(ld_e[u], 16)
                    sp.dma_start(wdn_sb[:, u, :, :], dn_v[bass.ds(e, 1)].rearrange("a p c d -> p (a c) d")).then_inc(ld_e[u], 16)
                    if g == 0 and u == 0:
                        sp.wait_ge(dispatched, (1 + B * T * TOPK) * 16)
                    sp.dma_start(xg[:, u, :, :], xs[bass.ds(r, SLOTS), :].rearrange("(a p) w -> p a w", p=P)).then_inc(ld_e[u], 16)

            load(0)
            with sp.Fori(0, GROUPS - 1) as i:
                load((i, 1))
            for u in range(DEPTH):
                sp.wait_ge(scattered[u], GROUPS * HALVES * 16)
            y_v = ys.rearrange("(k n p) d -> p k n d", k=TOPK, p=P)
            for c in range(NT // FOUT):
                for k in range(TOPK):
                    n = slice(c * FOUT, (c + 1) * FOUT)
                    sp.dma_start(y3[c][:, k, :, :], y_v[:, k, n, :]).then_inc(ld_y[c], 16)
            out_v = out.rearrange("b (t p) d -> p (b t) d", p=P)
            for c in range(NT // FOUT):
                n = slice(c * FOUT, (c + 1) * FOUT)
                sp.wait_ge(f_out, c + 1)
                sp.dma_start(out_v[:, n, :], x_all[:, n, :]).then_inc(stored, 16)
            sp.wait_ge(stored, 16 * (NT // FOUT))

        @block.gpsimd
        def _(pool):
            pool.memset(ident[:, :], 0.0).then_inc(p_chain, 1)
            pool.wait_ge(p_chain, 1)
            pool.affine_select(out=ident[:, :], in_=ident[:, :], compare_op=ALU.not_equal, fill=1.0, base=0,
                               pattern=[[-1, P]], channel_multiplier=1).then_inc(consts, 1)
            pool.memset(ident16[:, :], 0.0).then_inc(p_chain, 1)
            pool.memset(mask16[:, :, :], 0.0).then_inc(p_chain, 1)
            pool.memset(tri[:, :], 1.0).then_inc(p_chain, 1)
            pool.memset(tri16[:, :], 1.0).then_inc(p_chain, 1)
            pool.memset(upto[:, :, :], 1.0).then_inc(p_chain, 1)
            pool.wait_ge(p_chain, 6)
            pool.affine_select(out=ident16[:, :], in_=ident16[:, :], compare_op=ALU.not_equal, fill=1.0, base=0,
                               pattern=[[-1, P]], channel_multiplier=1).then_inc(consts, 1)
            pool.affine_select(out=mask16[:, :, :], in_=mask16[:, :, :], compare_op=ALU.is_ge, fill=NEG, base=0,
                               pattern=[[0, 2], [-1, P]], channel_multiplier=1).then_inc(consts, 1)
            for m in (tri, tri16):
                pool.affine_select(out=m[:, :], in_=m[:, :], compare_op=ALU.is_ge, fill=0.0, base=0,
                                   pattern=[[1, P]], channel_multiplier=-1).then_inc(consts, 1)
            exact = dict(allow_small_or_imprecise_dtypes=True)
            pool.iota(region[:, :], [[CAP, E]], base=0, channel_multiplier=0, **exact).then_inc(tables_ready, 1)
            pool.iota(steps256[:, :], [[SLOTS, N // SLOTS]], base=0, channel_multiplier=0, **exact).then_inc(tables_ready, 1)
            pool.iota(tau[:, :], [[1, TILES]], base=0, channel_multiplier=0, **exact).then_inc(tables_ready, 1)
            pool.iota(result_row[:, :, :], [[P, T], [N, TOPK]], base=0, channel_multiplier=1).then_inc(tables_ready, 1)
            pool.memset(padding[:, :, 0:D], 0.0).then_inc(tables_ready, 1)
            pool.iota(padding[:, :, D:ROW].bitcast(I32), [[0, PAD // P], [0, 1]], base=SKIP, channel_multiplier=0).then_inc(tables_ready, 1)
            pool.affine_select(out=upto[:, :, :], in_=upto[:, :, :], compare_op=ALU.is_ge, fill=0.0, base=0,
                               pattern=[[1, E], [-1, E]], channel_multiplier=0).then_inc(tables_ready, 1)
            pool.wait_ge(tables_ready, 6)
            pool.dma_start(xs[E * CAP:ROWS, :].rearrange("(a p) w -> p a w", p=P), padding[:, 0:SLOTS // P, :]).then_inc(dispatched, 16)
            pool.memset(spare_p[:, :], 0.0).then_inc(p_cell, 1)
            pool.wait_ge(ld_c, 48)
            LINKS = 3 + 1 + 3
            BASE = 6

            def rotate(b, link0, src, dst, which):
                c, s = tab[:, 2 * which], tab[:, 2 * which + 1]

                def pairs(a):
                    return a.rearrange("p t (n two) -> p t n two", two=2)
                pool.tensor_tensor(kq1[:, :, :], src[:, :, :], c, ALU.mult).then_inc(p_chain, 1)
                for a, o in ((0, 1), (1, 0)):
                    pool.tensor_tensor(pairs(kq2[:, :, :])[:, :, :, a], pairs(src[:, :, :])[:, :, :, o],
                                       pairs(s)[:, :, :, a], ALU.mult).then_inc(p_chain, 1)
                pool.wait_ge(p_chain, at(b, LINKS, BASE + link0 + 3))
                return pool.tensor_tensor(dst[:, :, :], kq1[:, :, :], kq2[:, :, :], ALU.add)

            def outer(b):
                pool.wait_ge(ld_ctx, at(b, 16, 16))
                wait(pool, pe_RET, at(b, 4, 0))
                rotate(b, 0, ctx_b, kt, 1).then_inc(p_chain, 1)
                pool.wait_ge(p_chain, at(b, LINKS, BASE + 4))
                for t in range(T):
                    k = kt[:, t, :].rearrange("p (h d) -> p h d", h=RH)
                    v = ctx_b[:, t, :].rearrange("p (h e) -> p h e", h=RH)
                    o = kv[:, t, :, :].rearrange("p a (h d e) -> p (a h) d e", d=RD, e=RD)
                    ins = pool.tensor_tensor(o, bc(k, 3, RD), bc(v, 2, RD), ALU.mult)
                ins.then_inc(p_kv, 1)

            def retained(b):
                for t in range(T):
                    for half in range(2):
                        pool.wait_ge(v_ret, at(b, 4, 2 * t + half + 1))
                        n = 2 * (2 * t + half)
                        q4, q2 = sum4[:, :, :], sum2[:, :, :]
                        pr = prod[:, half, :].rearrange("p (n d) -> p n d", d=RD)
                        pool.tensor_tensor(q4, pr[:, :, 0:4], pr[:, :, 4:8], ALU.add).then_inc(p_sum, 1)
                        pool.wait_ge(p_sum, at(b, 8, n + 1))
                        pool.tensor_tensor(q2, q4[:, :, 0:2], q4[:, :, 2:4], ALU.add).then_inc(p_sum, 1)
                        pool.wait_ge(p_sum, at(b, 8, n + 2))
                        pool.tensor_tensor(ret[:, t, half * 64:(half + 1) * 64], q2[:, :, 0], q2[:, :, 1], ALU.add).then_inc(p_ret, 1)

            def queries(b):
                pool.wait_ge(v_xn2, at(b, 1, 1))
                rotate(b, 4, xn2, qt, 0).then_inc(p_q, 1)

            def carry(n):
                return pool.tensor_tensor(spare_p[:, n:n + 1], tri[:, 0:1], tri[:, 0:1], ALU.mult)

            def pack(b):
                pool.wait_ge(v_xn3, at(b, 1, 1))
                wait(pool, dispatched, at(b, 16 * T * TOPK, 16))
                carry(0)
                for t in range(T):
                    ins = pool.tensor_copy(packed[:, t, :, 0:D], bc(xn3[:, t, :], 1, TOPK))
                ins.then_inc(p_pack, 1)

            def dispatch(b):
                if b == B - 1:
                    pool.wait_ge(padded, E * 16)
                pool.wait_ge(v_slot, at(b, 1, 1))
                pool.wait_ge(p_pack, at(b, 1, 1))
                carry(1)
                for t in range(T):
                    for k in range(TOPK):
                        pool.indirect_dma_start(
                            out=xs, out_offset=bass.IndirectOffsetOnAxis(ap=slot_i[:, t, k:k + 1], axis=0),
                            in_=packed[:, t, k, :], in_offset=None).then_inc(dispatched, 16)

            def keep(b):
                pool.wait_ge(v_x2, at(b, 1, 1))
                carry(2)
                pool.tensor_copy(x_all[:, bass.ds(tile_of(b, 0), T), :], x2b[:, :, :]).then_inc(p_keep, 1)

            outer(0)
            with pool.Fori(0, B - 1) as i:
                queries((i, 0))
                retained((i, 0))
                keep((i, 0))
                pack((i, 0))
                outer((i, 1))
                dispatch((i, 0))
            queries(B - 1)
            retained(B - 1)
            keep(B - 1)
            pack(B - 1)
            dispatch(B - 1)

            def send(g):
                for u in range(DEPTH):
                    pool.wait_ge(p_cell, at(g, DEPTH, u + 1))
                    pool.wait_ge(f_y, at(g, DEPTH, u + 1))
                    carry(3).then_inc(p_cell, 1)
                    for a in range(HALVES):
                        pool.indirect_dma_start(
                            out=ys, out_offset=bass.IndirectOffsetOnAxis(ap=row_i[:, u, a:a + 1], axis=0),
                            in_=y_sb[:, u, a, :], in_offset=None,
                            bounds_check=TOPK * N - 1, oob_is_err=False).then_inc(scattered[u], 16)

            with pool.Fori(0, GROUPS) as i:
                send((i, 0))

        @block.scalar
        def _(act):
            def wT_out(s):
                act.wait_ge(pw_T, s + 1)
                act.activation(wT[:, s % 2, :, :].rearrange("p a d -> p (a d)"), tb[s % 2][:, 0:2 * P], ACT.Copy).then_inc(aw_T, 1)

            wT_out(0)
            for s in range(PAIRS):
                if s + 1 < PAIRS:
                    wT_out(s + 1)
                act.wait_ge(pw_A, s + 1)
                for h in range(2):
                    act.activation(a_sb[:, 2 * s + h, :], pair_bank[s % 2][h][:, 0:P], ACT.Copy)
                    ins = act.activation(a_hi[:, 2 * s + h, :], pair_bank[s % 2][h][:, 0:P], ACT.Copy)
                ins.then_inc(aw_A, 1)
            act.wait_ge(pw_A, PAIRS + 1)
            act.activation(bup_sb[:, :, :].rearrange("p e c -> p (e c)"), s0[:, 0:E * HC], ACT.Copy).then_inc(aw_A, 1)
            act.wait_ge(ld_w, 32)
            act.activation(wv_hi[:, :], wkv_sb[:, H * DH:], ACT.Copy).then_inc(a_hi_wv, 1)
            act.wait_ge(ld_c, 48)

            def xT_out(b):
                act.wait_ge(pe_XT, at(b, 1, 1))
                act.activation(xN[:, :], zb[:, S:2 * S], ACT.Copy, scale=normw_sb[:, 0:1])
                act.activation(xN_hi[:, :], zb[:, S:2 * S], ACT.Copy, scale=normw_sb[:, 0:1]).then_inc(a_xN, 1)

            def next_x(b):
                act.wait_ge(v_xlo, at(b, 1, 1))
                if b != 0:
                    act.wait_ge(pe_S, at(back(b), PAIRS, PAIRS))
                act.activation(xT_hi[:, :], xN_hi[:, :], ACT.Copy)
                act.activation(xT_lo[:, :], xN_lo[:, :], ACT.Copy).then_inc(a_xT, 1)

            def z_out(b, s):
                act.wait_ge(pe_Z, at(b, PAIRS, s + 1))
                act.activation(z_hi[:, :, :].rearrange("p h j -> p (h j)"), zb[:, :], ACT.Copy).then_inc(a_z, 1)

            def probs(b, s):
                act.wait_ge(v_nm, at(b, PAIRS, s + 1))
                w = s % 2
                for h in range(2):
                    act.activation(p_sb[:, w, h, 0:P], s0[:, h * P:(h + 1) * P], ACT.Exp,
                                   bias=nmx[:, w, 0, h:h + 1], scale=SCALE)
                    ins = act.activation(p_sb[:, w, h, P:3 * P], s1[w][:, h * S:(h + 1) * S], ACT.Exp,
                                         bias=nmx[:, w, 1, h:h + 1], scale=SCALE)
                ins.then_inc(a_P, 1)

            def pT_out(b, s):
                act.wait_ge(pe_T, at(b, PAIRS, s + 1))
                for h in range(2):
                    ins = act.activation(pT[:, s % 2, h, :], tb[h][:, 0:BLOCKS * P], ACT.Copy)
                ins.then_inc(a_PT, 1)

            def oT_out(b, s):
                act.wait_ge(pe_OT, at(b, PAIRS, s + 1))
                act.activation(oT[:, s, :, :].rearrange("p t i -> p (t i)"), zb[:, 0:S], ACT.Copy).then_inc(a_oT, 1)

            def v_out(b, n, src, t, half):
                act.wait_ge(pe_V, at(b, 4, n))
                act.activation(v_sb[:, t, half * 8:half * 8 + 8, 0:DH], src[:, :].rearrange("p (h d) -> p h d", h=8), ACT.Copy).then_inc(a_V, 1)

            def step(cur, prev, nxt, s):
                if cur is not None and s + 1 < PAIRS:
                    z_out(cur, s + 1)
                elif cur is not None and nxt is not None:
                    z_out(nxt, 0)
                if prev is not None and s == 7:
                    act.wait_ge(pe_XN, at(prev, 1, 1))
                    act.activation(xn3T[:, :], xb[:, 0:S], ACT.Copy).then_inc(a_xn3T, 1)
                if (w := lagged(cur, prev, s, 1)) and (cur is not None or s < 1):
                    pT_out(*w)
                if cur is not None:
                    if s == 7 and nxt is not None:
                        next_x(nxt)
                    if s == 0:
                        act.wait_ge(pe_G, at(cur, 1, 1))
                        act.activation(gexp[:, :, :].rearrange("p t h -> p (t h)"), xb[:, 32:32 + T * H], ACT.Exp, scale=-1.0).then_inc(a_ge, 1)
                    probs(cur, s)
                if (w := lagged(cur, prev, s, 3)) and (cur is not None or s < 3):
                    oT_out(*w)
                if s == 3 and nxt is not None:
                    xT_out(nxt)
                if cur is not None:
                    if s == 1:
                        v_out(cur, 1, xb, 0, 0)
                        v_out(cur, 4, tb[1], 1, 0)
                if prev is not None:
                    if s == 7:
                        act.wait_ge(v_dl, at(prev, 1, 1))
                        act.activation(el[:, :, :], dl[:, :, :], ACT.Exp).then_inc(a_el, 1)

            xT_out(0)
            z_out(0, 0)
            next_x(0)
            for s in range(PAIRS):
                step(0, None, 1, s)
            with act.Fori(0, B - 2) as i:
                for s in range(PAIRS):
                    step((i, 1), (i, 0), (i, 2), s)
            for s in range(PAIRS):
                step(B - 1, B - 2, None, s)
            for s in range(PAIRS):
                step(None, B - 1, None, s)
            def gelu(g, u):
                act.wait_ge(ld_b[u], at(g, 32, 32))
                for j in range(2):
                    act.wait_ge(f_up, at(g, 2 * DEPTH, 2 * u + j + 1))
                    for m in range(2):
                        n = 2 * j + m
                        ins = act.activation(hT[:, u % 2, n, :], (s1, tb)[u % 2][j][:, m * SLOTS:(m + 1) * SLOTS],
                                             ACT.Gelu, bias=bup_now[:, u, n:n + 1])
                    ins.then_inc(f_gelu, 1)

            def biases(g, u):
                t = (g[0] * DEPTH + (g[1] * DEPTH + u)) if isinstance(g, tuple) else g * DEPTH + u
                if g != 0:
                    act.wait_ge(f_y, at(back(g), DEPTH, u + 1))
                e = act.value_load(plan[0:1, 1, bass.ds(t, 1)], min_val=0, max_val=E - 1)
                act.dma_start(bup_now[:, u, :], bup_sb[:, bass.ds(e, 1), :].rearrange("p a c -> p (a c)")).then_inc(ld_b[u], 16)
                act.dma_start(bdn_now[:, u, :], f_bdown[bass.ds(e, 1), :].broadcast_to([P, D])).then_inc(ld_b[u], 16)

            def up_high(g, u):
                act.wait_ge(ld_e[u], at(g, 16 * 3, 16 * 3))
                act.activation(wup_hi[:, u % 2, :], wup_sb[:, u, :], ACT.Copy).then_inc(f_w, 1)

            def tiles(g, last):
                for u in range(DEPTH):
                    if u + 1 < DEPTH:
                        up_high(g, u + 1)
                    elif not last:
                        up_high(after(g), 0)
                    gelu(g, u)
                    if u + AHEAD < DEPTH:
                        biases(g, u + AHEAD)
                    elif not last:
                        biases(after(g), u + AHEAD - DEPTH)

            act.wait_ge(v_plan, 1)
            for u in range(AHEAD):
                biases(0, u)
            up_high(0, 0)
            tiles(0, False)
            with act.Fori(0, GROUPS - 2) as i:
                tiles((i, 1), False)
            tiles(GROUPS - 1, True)

        @block.tensor
        def _(pe):
            pe.wait_ge(consts, 1)
            pe.wait_ge(ld_w, 32)
            def weights_T(s):
                wait(pe, aw_T, s - 1)
                for q, w in ((0, wq_sb), (1, wkv_sb)):
                    ins = pe.transpose(tb[s % 2][:, q * P:(q + 1) * P], w[:, s * P:(s + 1) * P], ident[:, :])
                ins.then_inc(pw_T, 1)

            weights_T(0)
            for s in range(PAIRS):
                if s + 1 < PAIRS:
                    weights_T(s + 1)
                pe.wait_ge(aw_T, s + 1)
                wait(pe, aw_A, s - 1)
                for h in range(2):
                    r = slice(h * DH, (h + 1) * DH)
                    ins = pe.matmul(pair_bank[s % 2][h][:, 0:P], wT[r, s % 2, 1, :], wT[r, s % 2, 0, :],
                                    start=True, stop=True)
                ins.then_inc(pw_A, 1)
            pe.wait_ge(aw_A, PAIRS)
            pe.wait_ge(consts, 5)
            pe.wait_ge(consts_v, 5)
            pe.wait_ge(ld_c, 48)
            pe.wait_ge(ld_wo, 48)
            pe.transpose(s0[:, 0:E * HC], bup_rows[:, :], ident[0:E * HC, 0:E * HC]).then_inc(pw_A, 1)
            pe.wait_ge(aw_A, PAIRS + 1)

            def x_T(b):
                pe.wait_ge(v_xrn, at(b, 1, 1))
                for t in range(T):
                    ins = pe.transpose(zb[:, S + t * P:S + (t + 1) * P], xrn[:, t, :], ident[:, :])
                ins.then_inc(pe_XT, 1)

            def split_product(o, lhs, rhs, last):
                for n, (l, m) in enumerate(((0, 0), (0, 1), (1, 0))):
                    ins = pe.matmul(o, lhs[l], rhs[m], start=(n == 0), stop=(last and n == 2), skip_group_check=True)
                return ins

            def z_of(b, s, turned, nxt):
                wait(pe, a_oT, turned)
                if s == 0:
                    pe.wait_ge(v_xlo, at(b, 1, 1))
                if s == 1:
                    pe.wait_ge(a_xT, at(b, 1, 1))
                if nxt is not None and s == 5:
                    pe.wait_ge(a_xN, at(nxt, 1, 1))
                if b == 0 and s < 2:
                    pe.wait_ge(v_split, s + 1)
                wait(pe, v_z, at(b, PAIRS, s))
                if s == 3:
                    pe.wait_ge(v_V, at(b, 2, 1))
                for h in range(2):
                    ins = split_product(zb[:, h * S:(h + 1) * S], (a_hi[:, 2 * s + h, :], a_lo[:, 2 * s + h, :]),
                                        (xT_hi[:, :], xT_lo[:, :]) if s else (xN_hi[:, :], xN_lo[:, :]), True)
                ins.then_inc(pe_Z, 1)

            def scores(b, s):
                pe.wait_ge(v_z, at(b, PAIRS, s + 1))
                if s == 0:
                    pe.wait_ge(a_xT, at(b, 1, 1))
                wait(pe, a_P, at(b, PAIRS, s - 1))
                w = s % 2
                s1v = s1[w][:, :].rearrange("p (h j) -> p h j", h=2)
                s0v = s0[:, 0:S].rearrange("p (h j) -> p h j", h=2)
                split_product(s1v, (xT_hi[:, P:2 * P], xT_lo[:, P:2 * P]), (z_hi[:, :, :], z_lo[:, :, :]), False)
                pe.matmul(s1v[:, :, P:2 * P], ident16[:, :], mask16[:, :, :], start=False, stop=True, skip_group_check=True)
                wait(pe, a_P, at(b, PAIRS, s))
                split_product(s0v, (xT_hi[:, 0:P], xT_lo[:, 0:P]), (z_hi[:, :, 0:P], z_lo[:, :, 0:P]), False)
                pe.matmul(s0v, ident16[:, :], mask16[:, :, :], start=False, stop=True, skip_group_check=True).then_inc(pe_S, 1)

            def turn(b, s):
                pe.wait_ge(a_P, at(b, PAIRS, s + 1))
                wait(pe, a_PT, at(b, PAIRS, s))
                if s == 1:
                    pe.wait_ge(v_V, at(b, 2, 2))
                    pe.wait_ge(a_V, at(b, 2, 2))
                for h in range(2):
                    for k in range(BLOCKS):
                        ins = pe.transpose(tb[h][:, k * P:(k + 1) * P], p_sb[:, s % 2, h, k * P:(k + 1) * P], ident[:, :])
                ins.then_inc(pe_T, 1)

            def weigh(b, s):
                pe.wait_ge(a_PT, at(b, PAIRS, s + 1))
                wait(pe, v_norm, at(b, PAIRS, s))
                if s == 0:
                    pe.wait_ge(v_V, at(b, 2, 2))
                    pe.wait_ge(a_V, at(b, 2, 2))
                for h in range(2):
                    for qt_, blocks in ((0, (0,)), (1, (1, 2))):
                        for n, k in enumerate(blocks):
                            c = (qt_ * 2 + h) * VW
                            ins = pe.matmul(ob[:, c:c + VW], pT[:, s % 2, h, k * P:(k + 1) * P],
                                            v_sb[:, n, 2 * s + h, :], start=(n == 0), stop=(n == len(blocks) - 1))
                ins.then_inc(pe_PV, 1)

            def o_turn(b, s, z_out_of, nxt):
                pe.wait_ge(v_norm, at(b, PAIRS, s + 1))
                wait(pe, v_z, z_out_of)
                wait(pe, a_oT, at(b, PAIRS, s))
                if nxt is not None:
                    x_T(nxt)
                for t in range(T):
                    ins = pe.transpose(zb[:, t * P:(t + 1) * P], o_sb[:, s % 2, t, :], ident[:, :])
                ins.then_inc(pe_OT, 1)

            def gates(b, older):
                if older is not None:
                    pe.wait_ge(v_lg, at(older, 1, 1))
                for t in range(T):
                    ins = pe.matmul(xb[:, 32 + t * H:32 + (t + 1) * H], xN[:, t * P:(t + 1) * P], wg_sb[:, :], start=True, stop=True)
                ins.then_inc(pe_G, 1)

            def values(b, prev):
                pe.wait_ge(a_ge, at(b, 1, 1))
                if prev is not None:
                    pe.wait_ge(v_filled, at(prev, 1, 1))
                if b == 0:
                    pe.wait_ge(v_split, 3)
                plan = ((xb, 0, 0), (zb, 1, 1), (tb[0], 0, 1), (tb[1], 1, 0))
                for n, (dst, t, half) in enumerate(plan):
                    if n == 1:
                        pe.wait_ge(v_z, at(b, PAIRS, 3))
                        if prev is not None:
                            pe.wait_ge(a_oT, at(prev, PAIRS, 7))
                    if n == 2:
                        pe.wait_ge(a_PT, at(b, PAIRS, 1))
                    c, k = slice(t * P, (t + 1) * P), slice(half * 512, half * 512 + 512)
                    split_product(dst[:, :], (xT_hi[:, c], xT_lo[:, c]), (wv_hi[:, k], wv_lo[:, k]), True).then_inc(pe_V, 1)

            def project(cur, b, pairs):
                if cur is not None:
                    pe.wait_ge(a_V, at(cur, 2, 1))
                else:
                    pe.wait_ge(v_filled, at(b, 1, 1))
                pe.wait_ge(a_oT, at(b, PAIRS, pairs[-1] + 1))
                for t in range(T):
                    for s in pairs:
                        ins = pe.matmul(xb[:, t * P:(t + 1) * P], oT[:, s, t, :], wout_sb[:, s, :],
                                        start=(t == 0 and s == 0), stop=(s == PAIRS - 1), skip_group_check=True)
                return ins

            def state(b, t, half):
                n = 2 * t + half
                if n == 0:
                    pe.wait_ge(v_x1, at(b, 1, 1))
                    pe.wait_ge(p_kv, at(b, 1, 1))
                else:
                    pe.wait_ge(v_ret, at(b, 4, n))
                if t:
                    pe.matmul(xb[:, :], ones[:, :], kv[:, 0, half, :], start=True, stop=False)
                pe.matmul(xb[:, :], tri[:, :], kv[:, t, half, :], start=(t == 0), stop=True).then_inc(pe_RET, 1)

            def ffn_in(b):
                pe.wait_ge(v_xc3, at(b, 1, 1))
                pe.wait_ge(v_ret, at(b, 4, 4))
                for t in range(T):
                    ins = pe.transpose(xb[:, t * P:(t + 1) * P], xc3[:, t, :], ident[:, :])
                ins.then_inc(pe_XN, 1)

            def logits(b):
                pe.wait_ge(a_xn3T, at(b, 1, 1))
                for t in range(T):
                    ins = pe.matmul(xb[:, t * E:(t + 1) * E], xn3T[:, t * P:(t + 1) * P], fwg_sb[:, :], start=True, stop=True)
                ins.then_inc(pe_LG, 1)

            def counts(cur, b):
                pe.wait_ge(v_hit, at(b, 1, 1))
                if cur is not None:
                    pe.wait_ge(a_ge, at(cur, 1, 1))
                o = [xb[:, 64 + n * E:64 + (n + 1) * E] for n in range(3)]
                pe.matmul(o[0], tri16[:, :], hit16[:, 0, :], start=True, stop=True)
                pe.matmul(o[1], ones16[:, :], hit16[:, 0, :], start=True, stop=False)
                pe.matmul(o[1], tri16[:, :], hit16[:, 1, :], start=False, stop=True)
                pe.matmul(o[2], ones16[:, :], hit16[:, 0, :], start=True, stop=False)
                pe.matmul(o[2], ones16[:, :], hit16[:, 1, :], start=False, stop=True).then_inc(pe_CNT, 1)

            def step(cur, prev, nxt, older, s):
                if cur is not None:
                    scores(cur, s)
                if prev is not None:
                    if s == 3:
                        project(cur, prev, [PAIRS - 1]).then_inc(pe_OUT, 1)
                    if s in (4, 5):
                        state(prev, s - 4, 0)
                done = at(prev, PAIRS, PAIRS + s - 3) if s < 4 and prev is not None else at(cur, PAIRS, s - 3) if cur is not None else 0
                z_seen = 0 if prev is None else at(prev, PAIRS, PAIRS)
                if cur is not None and s + 1 < PAIRS:
                    z_of(cur, s + 1, done, nxt)
                    z_seen = at(cur, PAIRS, s + 2)
                elif cur is not None:
                    z_seen = at(cur, PAIRS, PAIRS)
                    if nxt is not None:
                        z_of(nxt, 0, done, None)
                        z_seen = at(nxt, PAIRS, 1)
                if cur is not None and s == 0:
                    gates(cur, older)
                if prev is not None and s == 7:
                    ffn_in(prev)
                if (w := lagged(cur, prev, s, 1)) and (cur is not None or s < 1):
                    turn(*w)
                if prev is not None and s == 2:
                    project(cur, prev, list(range(PAIRS - 1)))
                if prev is not None and s == 7:
                    logits(prev)
                if (w := lagged(cur, prev, s, 2)) and (cur is not None or s < 2):
                    weigh(*w)
                if (w := lagged(cur, prev, s, 3)) and (cur is not None or s < 3):
                    o_turn(*w, z_seen, nxt if s == 3 else None)
                if cur is not None:
                    if s == 1:
                        values(cur, prev)
                if prev is not None:
                    if s in (4, 5):
                        state(prev, s - 4, 1)
                if older is not None:
                    counts(cur, older)

            def batch(cur, prev, nxt):
                for s in range(1, PAIRS):
                    step(cur, prev, nxt, None, s)
                step(nxt, cur, None, prev, 0)

            x_T(0)
            z_of(0, 0, 0, None)
            step(0, None, 1, None, 0)
            batch(0, None, 1)
            with pe.Fori(0, B - 2) as i:
                batch((i, 1), (i, 0), (i, 2))
            batch(B - 1, B - 2, None)
            batch(None, B - 1, None)


            def turn_tokens(g, u):
                pe.wait_ge(ld_e[u], at(g, 16 * 3, 16 * 3))
                wait(pe, f_xg, at(g, DEPTH, u - 1))
                for a in range(HALVES):
                    ins = pe.transpose((xb, s0)[u % 2][:, a * P:(a + 1) * P], xg[:, u, a, 0:D], ident[:, :])
                ins.then_inc(f_T, 1)

            def up(g, u):
                pe.wait_ge(f_xg, at(g, DEPTH, u + 1))
                wait(pe, f_gelu, at(g, 2 * DEPTH, 2 * (u - 1)))
                for n in range(HC):
                    c = slice(n * P, (n + 1) * P)
                    ins = split_product((s1, tb)[u % 2][n // 2][:, (n % 2) * SLOTS:(n % 2 + 1) * SLOTS],
                                        (wup_hi[:, u % 2, c], wup_lo[:, u % 2, c]),
                                        (xgT_hi[:, u % 2, :], xgT_lo[:, u % 2, :]), True)
                    if n % 2:
                        ins.then_inc(f_up, 1)

            def down(g, u):
                pe.wait_ge(f_gelu, at(g, 2 * DEPTH, 2 * (u + 1)))
                wait(pe, f_y, at(g, DEPTH, u - 1))
                for a in range(HALVES):
                    for n in range(HC):
                        ins = pe.matmul((zb, ob)[u % 2][:, a * D:(a + 1) * D], hT[:, u % 2, n, a * P:(a + 1) * P],
                                        wdn_sb[:, u, n, :], start=(n == 0), stop=(n == HC - 1))
                ins.then_inc(f_dn, 1)

            def tiles(g, first, last):
                for u in range(DEPTH):
                    if u < DEPTH - 1:
                        turn_tokens(g, u + 1)
                    elif not last:
                        turn_tokens(after(g), 0)
                    up(g, u)
                    if u:
                        down(g, u - 1)
                    elif not first:
                        down(back(g), DEPTH - 1)

            turn_tokens(0, 0)
            tiles(0, True, False)
            with pe.Fori(0, GROUPS - 2) as i:
                tiles((i, 1), False, False)
            tiles(GROUPS - 1, False, True)
            down(GROUPS - 1, DEPTH - 1)

        @block.vector
        def _(dve):
            dve.memset(ones[:, :], 1.0).then_inc(consts_v, 1)
            dve.memset(v_sb[:, :, :, DH:VW], 1.0).then_inc(consts_v, 1)
            dve.memset(lg[:, :, E:LGW], NEG).then_inc(consts_v, 1)
            dve.memset(pick[:, :, TOPK:MAX8], NEG).then_inc(consts_v, 1)
            dve.memset(ones16[:, :], 1.0).then_inc(consts_v, 1)
            dve.wait_ge(tables_ready, 7)
            dve.tensor_copy(filled[:, :], region[:, :]).then_inc(v_filled, 1)

            def rsqrt(link, out_, val, n):
                y, a, t = nwy[:, 0:n], nwa[:, 0:n], nwt[:, 0:n]
                link(dve.tensor_single_scalar(t.bitcast(I32), val.bitcast(I32), 1, ALU.logical_shift_right))
                link(dve.tensor_scalar(y.bitcast(I32), t.bitcast(I32), -1.0, MAGIC, ALU.mult, ALU.add))
                for k in range(3):
                    link(dve.scalar_tensor_tensor(a, y, -0.5, y, ALU.mult, ALU.mult))
                    link(dve.scalar_tensor_tensor(t, a, 1.0, val, ALU.mult, ALU.mult))
                    link(dve.scalar_tensor_tensor(y if k < 2 else out_, t, 1.5, y, ALU.add, ALU.mult))

            n1 = [0]

            def link1(ins):
                n1[0] += 1
                ins.then_inc(stat1, 1)
                dve.wait_ge(stat1, n1[0])

            dve.wait_ge(ld_x, 16)
            for n in range(NT):
                ins = dve.bn_stats(st6[:, n, :], x_all[:, n, :])
            link1(ins)
            for n in range(NT):
                ins = dve.bn_aggr(mv[:, n, :], st6[:, n, :])
            link1(ins)
            link1(dve.tensor_scalar(r_ln[:, :], mv[:, :, 1], LN_EPS, None, ALU.add))
            rsqrt(link1, r_ln[:, :], r_ln[:, :], NT)
            link1(dve.tensor_tensor(ms[:, :], r_ln[:, :], r_ln[:, :], ALU.mult))
            link1(dve.tensor_tensor(rs1[:, :], ms[:, :], mv[:, :, 1], ALU.mult))
            link1(dve.tensor_scalar(ms[:, :], rs1[:, :], RMS_EPS, None, ALU.add))
            rsqrt(link1, ms[:, :], ms[:, :], NT)
            link1(dve.tensor_tensor(rs1[:, :], ms[:, :], r_ln[:, :], ALU.mult))

            CHAIN = 66
            sent = [0]

            def chain(i=None):
                def link(ins, carry=False):
                    sent[0] += 1
                    ins.then_inc(v_chain, 1)
                    dve.wait_ge(v_chain, sent[0] if i is None else i * CHAIN + sent[0])
                    if carry:
                        dve.memset(spare[:, :], 0.0)
                return link

            def norm_in(b):
                wait(dve, pe_XT, at(b, 1, 0))
                for t in range(T):
                    n = tile_of(b, t)
                    ins = dve.tensor_scalar(xrn[:, t, :], x_all[:, bass.ds(n, 1), :].rearrange("p a d -> p (a d)"),
                                            mv[:, bass.ds(n, 1), 0], rs1[:, bass.ds(n, 1)], ALU.subtract, ALU.mult)
                ins.then_inc(v_xrn, 1)

            def maxima(b, s, link):
                dve.wait_ge(pe_S, at(b, PAIRS, s + 1))
                w = s % 2
                dve.tensor_reduce(mx[:, w, 0, :], s0[:, 0:S].rearrange("p (h j) -> p h j", h=2), AX.X, ALU.max)
                link(dve.tensor_reduce(mx[:, w, 1, :], s1[w][:, :].rearrange("p (h j) -> p h j", h=2), AX.X, ALU.max))
                dve.tensor_scalar(nmx[:, w, :, :], mx[:, w, :, :], -SCALE, None, ALU.mult).then_inc(v_nm, 1)

            def x_low(b):
                dve.wait_ge(a_xN, at(b, 1, 1))
                dve.tensor_tensor(xN_lo[:, :], xN[:, :], xN_hi[:, :], ALU.subtract).then_inc(v_xlo, 1)

            def z_low(b, s):
                dve.wait_ge(a_z, at(b, PAIRS, s + 1))
                dve.tensor_tensor(z_lo[:, :, :].rearrange("p h j -> p (h j)"), zb[:, :], z_hi[:, :, :].rearrange("p h j -> p (h j)"),
                                  ALU.subtract).then_inc(v_z, 1)

            def normalise(b, s, link):
                if s == 0:
                    dve.wait_ge(a_ge, at(b, 1, 1))
                    link(dve.tensor_scalar(gate1[:, :, :], gexp[:, :, :], 1.0, None, ALU.add))
                    link(dve.reciprocal(gate[:, :, :], gate1[:, :, :]))
                dve.wait_ge(pe_PV, at(b, PAIRS, s + 1))
                o = ob[:, 0:4 * VW].rearrange("p (t h v) -> p t h v", t=T, h=2)
                link(dve.reciprocal(rr[:, :, :], o[:, :, :, DH]))
                link(dve.tensor_tensor(rg[:, :, :], rr[:, :, :], gate[:, :, 2 * s:2 * s + 2], ALU.mult))
                dve.tensor_tensor(o_sb[:, s % 2, :, :].rearrange("p t (h v) -> p t h v", h=2), o[:, :, :, 0:DH],
                                  bc(rg[:, :, :], 3, DH), ALU.mult).then_inc(v_norm, 1)

            def v_out(b, n, src, t, half):
                dve.wait_ge(pe_V, at(b, 4, n))
                dve.tensor_copy(v_sb[:, t, half * 8:half * 8 + 8, 0:DH], src[:, :].rearrange("p (h d) -> p h d", h=8)).then_inc(v_V, 1)

            def centre(link, src, dst):
                for t in range(T):
                    ins = dve.bn_stats(bst[:, t, :], src[:, t, :])
                link(ins, carry=True)
                for t in range(T):
                    ins = dve.bn_aggr(bmv[:, t, :], bst[:, t, :])
                link(ins)
                for t in range(T):
                    ins = dve.tensor_scalar(dst[:, t, :], src[:, t, :], bmv[:, t, 0:1], None, ALU.subtract)
                return ins

            def deviation(link, dst):
                link(dve.tensor_scalar(dst[:, :], bmv[:, :, 1], LN_EPS, None, ALU.add))
                rsqrt(link, dst[:, :], dst[:, :], T)

            def first_residual(b, link):
                dve.wait_ge(pe_OUT, at(b, 1, 1))
                ins = dve.tensor_tensor(x1b[:, :, :], x_all[:, bass.ds(tile_of(b, 0), T), :],
                                        xb[:, 0:S].rearrange("p (t d) -> p t d", t=T), ALU.add)
                ins.then_inc(v_x1, 1)
                dve.wait_ge(v_x1, at(b, 1, 1))
                centre(link, x1b, xn2).then_inc(v_xn2, 1)

            def read_state(b, t, half):
                n = 2 * t + half
                dve.wait_ge(pe_RET, at(b, 4, n + 1))
                if n == 0:
                    dve.wait_ge(p_q, at(b, 1, 1))
                if n >= 2:
                    dve.wait_ge(p_ret, at(b, 4, n - 1))
                q = qt[:, t, half * 64:(half + 1) * 64].rearrange("p (h d) -> p h d", h=8)
                dve.tensor_tensor(prod[:, half, :].rearrange("p (h e d) -> p h e d", h=8, e=RD),
                                  xb[:, :].rearrange("p (h d e) -> p h e d", h=8, d=RD),
                                  bc(q, 2, RD), ALU.mult).then_inc(v_ret, 1)

            def second_residual(b, link):
                dve.wait_ge(p_ret, at(b, 4, 4))
                for t in range(T):
                    ins = dve.scalar_tensor_tensor(x2b[:, t, :], ret[:, t, :], brs[:, t:t + 1], x1b[:, t, :], ALU.mult, ALU.add)
                ins.then_inc(v_x2, 1)
                dve.wait_ge(v_x2, at(b, 1, 1))
                centre(link, x2b, xc3).then_inc(v_xc3, 1)

            def scale_third():
                for t in range(T):
                    ins = dve.tensor_scalar(xn3[:, t, :], xc3[:, t, :], brs3[:, t:t + 1], None, ALU.mult)
                ins.then_inc(v_xn3, 1)

            def route_a(b, link):
                dve.wait_ge(pe_LG, at(b, 1, 1))
                dve.tensor_tensor(lg[:, :, 0:E], xb[:, 0:T * E].rearrange("p (t e) -> p t e", t=T),
                                  bc(brs3[:, :], 2, E), ALU.mult).then_inc(v_lg, 1)
                dve.wait_ge(consts_v, 4)
                dve.wait_ge(v_lg, at(b, 1, 1))
                for t in range(T):
                    ins = dve.max(top[:, t, :], lg[:, t, :])
                link(ins)
                dve.tensor_tensor(dl[:, :, :], lg[:, :, 0:E], bc(top[:, :, 0], 2, E), ALU.subtract).then_inc(v_dl, 1)

            def choose(link):
                link(dve.tensor_copy(pick[:, :, 0:TOPK], top[:, :, 0:TOPK]), carry=True)
                for t in range(T):
                    ins = dve.match_replace(rep[:, t, :], pick[:, t, :], lg[:, t, :], FOUND)
                link(ins)
                dve.tensor_single_scalar(hit16[:, :, :], rep[:, :, 0:E], FOUND, ALU.is_equal).then_inc(v_hit, 1)
                link(dve.tensor_single_scalar(hit[:, :, :], rep[:, :, 0:E], FOUND, ALU.is_equal))

            def route_b(b, link):
                dve.wait_ge(a_el, at(b, 1, 1))
                link(dve.tensor_tensor(hw[:, :, :], hit[:, :, :], el[:, :, :], ALU.mult))
                link(dve.tensor_reduce(es[:, :], hw[:, :, :], AX.X, ALU.add))
                link(dve.reciprocal(er[:, :], es[:, :]))
                dve.tensor_tensor(cwb[:, :, :], hw[:, :, :], bc(er[:, :], 2, E), ALU.mult)
                dve.wait_ge(pe_CNT, at(b, 1, 1))
                link(dve.tensor_tensor(place[:, :, :], xb[:, 64:64 + T * E].rearrange("p (t e) -> p t e", t=T),
                                       bc(filled[:, :], 1, T), ALU.add))
                dve.tensor_tensor(slot1[:, :, :], place[:, :, :], hit[:, :, :], ALU.mult)
                dve.tensor_tensor(filled[:, :], filled[:, :], xb[:, 64 + T * E:64 + 3 * E], ALU.add).then_inc(v_filled, 1)

            def route_c(b, link):
                dve.wait_ge(v_filled, at(b, 1, 2))
                dve.memset(spare[:, :], 0.0)
                for t in range(T):
                    ins = dve.max(last3[:, t, :], slot1[:, t, :])
                wait(dve, dispatched, at(b, 16 * T * TOPK, 16))
                link(ins)
                dve.tensor_scalar(slot_i[:, :, :], last3[:, :, 0:TOPK], -1.0, None, ALU.add)
                link(dve.tensor_tensor(same[:, :, :, :], bc(slot1[:, :, :], 2, TOPK), bc(last3[:, :, 0:TOPK], 3, E), ALU.is_equal))
                dve.tensor_copy(packed[:, :, :, D].bitcast(I32), result_row[:, :, :]).then_inc(v_slot, 1)
                link(dve.tensor_tensor(samew[:, :, :, :], same[:, :, :, :], bc(cwb[:, :, :], 2, TOPK), ALU.mult))
                dve.tensor_scalar(result_row[:, :, :], result_row[:, :, :], float(S), None, ALU.add)
                link(dve.tensor_reduce(w3_all[:, bass.ds(tile_of(b, 0), T), :], samew[:, :, :, :], AX.X, ALU.add))

            def step(cur, prev, nxt, older, s, link):
                if cur is not None:
                    maxima(cur, s, link)
                    if s + 1 < PAIRS:
                        z_low(cur, s + 1)
                    elif nxt is not None:
                        z_low(nxt, 0)
                    if s == 4 and nxt is not None:
                        x_low(nxt)
                if older is not None and s == 0:
                    choose(link)
                if older is not None and s == 1:
                    route_b(older, link)
                if prev is not None:
                    if s in (4, 5):
                        read_state(prev, s - 4, 0)
                    if s == 6:
                        second_residual(prev, link)
                    if s == 7:
                        deviation(link, brs3)
                        route_a(prev, link)
                if (cur is not None or prev is not None) and (w := lagged(cur, prev, s, 2)) and (cur is not None or s < 2):
                    normalise(*w, link)
                if cur is not None and s == 1:
                    v_out(cur, 2, zb, 1, 1)
                    v_out(cur, 3, tb[0], 0, 1)
                if prev is not None:
                    if s == 3:
                        first_residual(prev, link)
                    if s in (4, 5):
                        read_state(prev, s - 4, 1)
                    if s == 4:
                        deviation(link, brs)
                if older is not None and s == 0:
                    scale_third()
                if older is not None and s == 1:
                    route_c(older, link)

            def batch(cur, prev, nxt, link):
                for s in range(2, PAIRS):
                    step(cur, prev, nxt, None, s, link)
                    if s == 2 and nxt is not None:
                        norm_in(nxt)
                for s in range(2):
                    step(nxt, cur, None, prev, s, link)

            norm_in(0)
            dve.wait_ge(aw_A, 1)
            dve.tensor_tensor(a_lo[:, 0:2, :], a_sb[:, 0:2, :], a_hi[:, 0:2, :], ALU.subtract).then_inc(v_split, 1)
            x_low(0)
            dve.wait_ge(aw_A, PAIRS)
            dve.tensor_tensor(a_lo[:, 2:H, :], a_sb[:, 2:H, :], a_hi[:, 2:H, :], ALU.subtract).then_inc(v_split, 1)
            z_low(0, 0)
            dve.wait_ge(a_hi_wv, 1)
            dve.tensor_tensor(wv_lo[:, :], wkv_sb[:, H * DH:], wv_hi[:, :], ALU.subtract).then_inc(v_split, 1)
            step(0, None, None, None, 0, chain())
            step(0, None, None, None, 1, chain())
            batch(0, None, 1, chain())
            with dve.Fori(0, B - 2) as i:
                before = sent[0]
                batch((i, 1), (i, 0), (i, 2), chain(i))
                assert sent[0] - before == CHAIN, sent[0] - before
            sent[0] += (B - 3) * CHAIN
            batch(B - 1, B - 2, None, chain())
            dve.wait_ge(v_filled, B)
            dve.tensor_copy(pad_row[:, :], filled[:, :]).then_inc(v_pad, 1)
            batch(None, B - 1, None, chain())

            fin = [0]

            def linkp(ins):
                fin[0] += 1
                ins.then_inc(v_fin, 1)
                dve.wait_ge(v_fin, fin[0])

            linkp(dve.tensor_tensor(count[:, :], filled[:, :], region[:, :], ALU.subtract))
            M = N // SLOTS
            linkp(dve.tensor_tensor(more[:, :, :], bc(count[:, :], 2, M), bc(steps256[:, :], 1, E), ALU.is_gt))
            linkp(dve.tensor_reduce(tiles_of[:, :], more[:, :, :], AX.X, ALU.add))
            linkp(dve.tensor_tensor(uptot[:, :, :], upto[:, :, :], bc(tiles_of[:, :], 1, E), ALU.mult))
            linkp(dve.tensor_reduce(ends[:, :], uptot[:, :, :], AX.X, ALU.add))
            linkp(dve.tensor_tensor(past[:, :, :], bc(ends[:, :], 1, TILES), bc(tau[:, :], 2, E), ALU.is_le))
            linkp(dve.tensor_tensor(pastn[:, :, :], past[:, :, :], bc(ends[:, :], 1, TILES), ALU.mult))
            dve.tensor_reduce(eid[:, :], past[:, :, :], AX.X, ALU.add)
            linkp(dve.tensor_reduce(begun[:, :], pastn[:, :, :], AX.X, ALU.max))
            dve.tensor_scalar(plan[:, 1, :], eid[:, :], float(E - 1), None, ALU.min)
            linkp(dve.tensor_tensor(off[:, :], tau[:, :], begun[:, :], ALU.subtract))
            linkp(dve.tensor_scalar(off[:, :], off[:, :], float(SLOTS), None, ALU.mult))
            linkp(dve.scalar_tensor_tensor(row_f[:, :], eid[:, :], float(CAP), off[:, :], ALU.mult, ALU.add))
            dve.tensor_scalar(plan[:, 0, :], row_f[:, :], float(E * CAP), None, ALU.min).then_inc(v_plan, 1)


            def tokens(g, u):
                dve.wait_ge(f_T, at(g, DEPTH, u + 1))
                turned = (xb, s0)[u % 2][:, 0:SLOTS]
                dve.tensor_copy(xgT_hi[:, u % 2, :], turned).then_inc(f_hi, 1)
                dve.wait_ge(f_hi, at(g, DEPTH, u + 1))
                dve.tensor_tensor(xgT_lo[:, u % 2, :], turned, xgT_hi[:, u % 2, :], ALU.subtract)
                dve.wait_ge(f_w, at(g, DEPTH, u + 1))
                dve.tensor_tensor(wup_lo[:, u % 2, :], wup_sb[:, u, :], wup_hi[:, u % 2, :], ALU.subtract).then_inc(f_xg, 1)
                if g != 0:
                    dve.wait_ge(scattered[u], at(g, 16 * HALVES, 0))
                dve.tensor_copy(row_i[:, u, :], xg[:, u, :, D].bitcast(I32))

            def results(g, u):
                dve.wait_ge(f_dn, at(g, DEPTH, u + 1))
                dve.tensor_tensor(y_sb[:, u, :, :], (zb, ob)[u % 2][:, 0:HALVES * D].rearrange("p (a d) -> p a d", a=HALVES),
                                  bc(bdn_now[:, u, :], 1, HALVES), ALU.add).then_inc(f_y, 1)

            def tiles(g, first, last):
                for u in range(DEPTH):
                    if u < DEPTH - 1:
                        tokens(g, u + 1)
                    elif not last:
                        tokens(after(g), 0)
                    if u:
                        results(g, u - 1)
                    elif not first:
                        results(back(g), DEPTH - 1)

            tokens(0, 0)
            tiles(0, True, False)
            with dve.Fori(0, GROUPS - 2) as i:
                tiles((i, 1), False, False)
            tiles(GROUPS - 1, False, True)
            results(GROUPS - 1, DEPTH - 1)

            dve.wait_ge(p_keep, B)
            for c in range(NT // FOUT):
                dve.wait_ge(ld_y[c], 16 * TOPK)
                for k in range(TOPK):
                    for n in range(c * FOUT, (c + 1) * FOUT):
                        ins = dve.scalar_tensor_tensor(x_all[:, n, :], y3[c][:, k, n - c * FOUT, :], w3_all[:, n, k:k + 1], x_all[:, n, :],
                                                       ALU.mult, ALU.add)
                    if k < TOPK - 1:
                        linkp(ins)
                ins.then_inc(f_out, 1)


_INS = ['x', 'ctx_1024', 'L0_attn_norm_w', 'L0_attn_Wq', 'L0_attn_Wkv', 'L0_attn_Wout', 'L0_attn_Wg', 'L0_ffn_Wg',
        'L0_ffn_Wup', 'L0_ffn_bup', 'L0_ffn_Wdown', 'L0_ffn_bdown']


def kernel(**inputs):
    import concourse.bacc as bacc
    from concourse.bass_utils import run_bass_kernel_spmd

    nc = bacc.Bacc("TRN2", target_bir_lowering=False, num_devices=1)
    arrays, args = {}, []
    for name in _INS:
        arrays[f"in_{name}"] = np.ascontiguousarray(inputs[name])
    arrays["in_tables"] = retention_tables()
    for name, a in arrays.items():
        args.append(nc.dram_tensor(name, a.shape, mybir.dt.from_np(a.dtype), kind="ExternalInput").ap())
    args.append(nc.dram_tensor("out_0", (B, S, D), F32, kind="ExternalOutput").ap())
    decoder(nc, *args)
    r = run_bass_kernel_spmd(nc, [arrays], core_ids=[0])
    return r.results[0]["out_0"]
```
